# Optimizing a Trainium2 kernel written in Bass

```python
import numpy as np
import jax
import jax.numpy as jnp

def _softmax(x, axis=-1):
    return jax.nn.softmax(x, axis=axis)

def _gelu(x):
    return jax.nn.gelu(x, approximate=True)

def _silu(x):
    return jax.nn.silu(x)

def _sigmoid(x):
    return jax.nn.sigmoid(x)

def _layernorm(x, axis=-1, eps=1e-05):
    m = jnp.mean(x, axis=axis, keepdims=True)
    v = jnp.var(x, axis=axis, keepdims=True)
    return (x - m) / jnp.sqrt(v + eps)

def _scatter_add(tgt, idx, src, axis=0):
    return tgt.at[idx].add(src)

def _segment_sum(src, seg, n):
    return jax.ops.segment_sum(src, seg, n)
kernel_name = 'mk_seq_preln_d1_jaxref_r8_ea6a46'

def setup_inputs(seed: int=0):
    np.random.seed(seed)
    _w = jnp.asarray

    def _L0_attn_setup():
        import jax, jax.numpy as jnp
        import numpy as np
        NQ, NKV, HD, SW = (32, 8, 64, 64)
        QM = NQ // NKV

        def _rope_tables(L):
            inv_freq = (1.0 / 1024.0) ** jnp.linspace(0.0, 1.0, HD // 4)
            inv_freq = jnp.concatenate([inv_freq, jnp.zeros(HD // 4)])
            theta = jnp.arange(L, dtype=jnp.float32)[:, None] * inv_freq[None, :]
            return (jnp.cos(theta), jnp.sin(theta))

        def _apply_rope(x, cos, sin):
            x1, x2 = jnp.split(x, 2, axis=-1)
            return jnp.concatenate([x1 * cos + x2 * sin, -x1 * sin + x2 * cos], axis=-1)
        key = jax.random.key(seed)
        k1, k2, k3 = jax.random.split(key, 3)
        B, L, D = (1, 256, 256)
        x = jax.random.normal(k1, (B, L, D), jnp.float32)
        W_qkv = jax.random.normal(k2, (D, (NQ + 2 * NKV) * HD), jnp.float32) * 0.02
        W_out = jax.random.normal(k3, (NQ * HD, D), jnp.float32) * 0.02
        s = jnp.zeros((1, NKV, QM), jnp.float32)
        return {'x': x, 'W_qkv': W_qkv, 'W_out': W_out, 's': s}
    _L0_attn_in = _L0_attn_setup()

    def _L0_ffn_setup():
        import math
        import jax, jax.numpy as jnp
        import numpy as np
        NUM_EXPERTS = 8
        TOP_K = 2
        CAP_FACTOR = 1.25
        D_MODEL = 256
        D_HIDDEN = 1024
        B, S = (4, 256)
        key = jax.random.key(seed)
        ks = jax.random.split(key, 6)
        x = jax.random.normal(ks[0], (B, S, D_MODEL), dtype=jnp.float32)
        gating_w = jax.random.normal(ks[1], (D_MODEL, NUM_EXPERTS), dtype=jnp.float32) * (1.0 / math.sqrt(D_MODEL))
        w1 = jax.random.normal(ks[2], (NUM_EXPERTS, D_MODEL, D_HIDDEN), dtype=jnp.float32) * (1.0 / math.sqrt(D_MODEL))
        b1 = jnp.zeros((NUM_EXPERTS, D_HIDDEN), dtype=jnp.float32)
        w2 = jax.random.normal(ks[3], (NUM_EXPERTS, D_HIDDEN, D_MODEL), dtype=jnp.float32) * (1.0 / math.sqrt(D_HIDDEN))
        b2 = jnp.zeros((NUM_EXPERTS, D_MODEL), dtype=jnp.float32)
        return {'x': x, 'gating_w': gating_w, 'w1': w1, 'b1': b1, 'w2': w2, 'b2': b2}
    _L0_ffn_in = _L0_ffn_setup()
    _d = {'L0_attn_x': _L0_attn_in['x'], 'L0_attn_W_qkv': _L0_attn_in['W_qkv'], 'L0_attn_W_out': _L0_attn_in['W_out'], 'L0_attn_s': _L0_attn_in['s'], 'L0_ffn_gating_w': _L0_ffn_in['gating_w'], 'L0_ffn_w1': _L0_ffn_in['w1'], 'L0_ffn_b1': _L0_ffn_in['b1'], 'L0_ffn_w2': _L0_ffn_in['w2'], 'L0_ffn_b2': _L0_ffn_in['b2']}
    _x0 = _d['L0_attn_x']
    _d['L0_attn_x'] = jax.random.normal(jax.random.fold_in(jax.random.key(seed), 1), (4, 512, 256), dtype=_x0.dtype)
    del _x0
    return _d

def reference(L0_attn_x, L0_attn_W_qkv, L0_attn_W_out, L0_attn_s, L0_ffn_gating_w, L0_ffn_w1, L0_ffn_b1, L0_ffn_w2, L0_ffn_b2):

    def _L0_attn_ref(x, W_qkv, W_out, s):
        import jax, jax.numpy as jnp
        import numpy as np
        NQ, NKV, HD, SW = (32, 8, 64, 64)
        QM = NQ // NKV

        def _rope_tables(L):
            inv_freq = (1.0 / 1024.0) ** jnp.linspace(0.0, 1.0, HD // 4)
            inv_freq = jnp.concatenate([inv_freq, jnp.zeros(HD // 4)])
            theta = jnp.arange(L, dtype=jnp.float32)[:, None] * inv_freq[None, :]
            return (jnp.cos(theta), jnp.sin(theta))

        def _apply_rope(x, cos, sin):
            x1, x2 = jnp.split(x, 2, axis=-1)
            return jnp.concatenate([x1 * cos + x2 * sin, -x1 * sin + x2 * cos], axis=-1)
        B, L, D = x.shape
        proj = x @ W_qkv
        q, k, v = jnp.split(proj, (NQ * HD, (NQ + NKV) * HD), axis=-1)
        cos, sin = _rope_tables(L)
        q = _apply_rope(q.reshape(B, L, NKV, QM, HD), cos[None, :, None, None, :], sin[None, :, None, None, :])
        k = _apply_rope(k.reshape(B, L, NKV, HD), cos[None, :, None, :], sin[None, :, None, :])
        v = v.reshape(B, L, NKV, HD)
        sm_scale = 1.0 / jnp.sqrt(jnp.float32(HD))
        attn = jnp.einsum('bqhmd,bkhd->bhmqk', q, k) * sm_scale
        q_pos = jnp.arange(L)[:, None]
        k_pos = jnp.arange(L)[None, :]
        mask = (q_pos >= k_pos) & (q_pos < k_pos + SW)
        attn = jnp.where(mask, -jnp.inf, attn)
        sink = jnp.broadcast_to(s[:, :, :, None, None], attn.shape[:-1] + (1,))
        w = jax.nn.softmax(jnp.concatenate([attn, sink], axis=-1), axis=-1)[..., :-1]
        out = jnp.einsum('bhmqk,bkhd->bqhmd', w, v).reshape(B, L, NQ * HD)
        return out @ W_out

    def _L0_ffn_ref(x, gating_w, w1, b1, w2, b2):
        import math
        import jax, jax.numpy as jnp
        import numpy as np
        NUM_EXPERTS = 8
        TOP_K = 2
        CAP_FACTOR = 1.25
        D_MODEL = 256
        D_HIDDEN = 1024
        B, S = (4, 256)
        b, s, d = x.shape
        x_flat = x.reshape(-1, d)
        T = x_flat.shape[0]
        num_items = T * TOP_K
        capacity = int(math.ceil(num_items / NUM_EXPERTS * CAP_FACTOR))
        gates = jax.nn.softmax(x_flat @ gating_w, axis=-1)
        topk_w, topk_idx = jax.lax.top_k(gates, TOP_K)
        norm_w = topk_w / (jnp.sum(topk_w, axis=-1, keepdims=True) + 1e-08)
        flat_e = topk_idx.reshape(-1)
        flat_t = jnp.repeat(jnp.arange(T, dtype=jnp.int32), TOP_K)
        flat_w = norm_w.reshape(-1)
        onehot = (flat_e[:, None] == jnp.arange(NUM_EXPERTS)[None, :]).astype(jnp.int32)
        pos_all = jnp.cumsum(onehot, axis=0) - 1
        position = jnp.take_along_axis(pos_all, flat_e[:, None].astype(jnp.int32), axis=1)[:, 0]
        valid = position < capacity
        pos_scatter = jnp.where(valid, position, capacity)
        buf = jnp.zeros((NUM_EXPERTS, capacity, d), dtype=x.dtype)
        buf = buf.at[flat_e, pos_scatter].set(x_flat[flat_t], mode='drop')
        h = jnp.maximum(jnp.einsum('ecd,edh->ech', buf, w1) + b1[:, None, :], 0.0)
        out_e = jnp.einsum('ech,ehd->ecd', h, w2) + b2[:, None, :]
        pos_gather = jnp.minimum(position, capacity - 1)
        gathered = out_e[flat_e, pos_gather]
        w_eff = jnp.where(valid, flat_w, 0.0)
        out_flat = jnp.zeros_like(x_flat).at[flat_t].add(gathered * w_eff[:, None])
        return out_flat.reshape(b, s, d)
    x = L0_attn_x
    x = x + _L0_attn_ref(_layernorm(x, axis=-1), L0_attn_W_qkv, L0_attn_W_out, L0_attn_s)
    x = x + _L0_ffn_ref(_layernorm(x, axis=-1), L0_ffn_gating_w, L0_ffn_w1, L0_ffn_b1, L0_ffn_w2, L0_ffn_b2)
    return x

_drawn_inputs = setup_inputs


def setup_inputs(seed=0):
    import zlib

    import numpy as np

    out = dict(_drawn_inputs(seed))
    spreads = {'L0_attn_s': (0.0, 0.1), 'L0_ffn_b1': (0.0, 0.1), 'L0_ffn_b2': (0.0, 0.1)}
    factors = {}
    for name, (base, spread) in spreads.items():
        noise = np.random.default_rng([zlib.crc32(name.encode()), seed]).standard_normal(out[name].shape)
        drawn = base * np.exp(spread * noise) if base else spread * noise
        out[name] = jnp.asarray(drawn.astype(out[name].dtype))
    for name, factor in factors.items():
        out[name] = (out[name] * factor).astype(out[name].dtype)
    return out
```

```python
from contextlib import ExitStack

import concourse.bass as bass
from concourse import mybir
from concourse.alu_op_type import AluOpType as ALU

F32 = mybir.dt.float32
F32R = mybir.dt.float32r
U32 = mybir.dt.uint32
ACT = mybir.ActivationFunctionType
AX = mybir.AxisListType.X

P = 128
B, L, D = 4, 512, 256
T = B * L
TILES = T // P
TPB = L // P
KC = D // P
NKV, QM, HD = 8, 4, 64
NQ = NKV * QM
GROUPS = B * NKV
BAND = 64
GW = QM * HD + 2 * HD
RH = HD // 4
PAIRS = QM // 2
UNITS = QM * TPB
E, HID, CAP, TOPK = 8, 1024, 640, 2
HC = HID // P
SLOTT = CAP // P
HALF = CAP // 2
EPS = 1e-5
SCALE = HD ** -0.5
MASKED = -3.0e38
NOWHERE = 1.0e6
LAG = 4
RING = 8


def moe_layer(nc, x, w_qkv, w_out, sink, gate_w, w1, b1, w2, b2, rope, out):
    ctx = ExitStack()
    with ctx:
        slot_rows = nc.dram_tensor("slot_rows", (E * CAP, D), F32, kind="Internal").ap()
        expert_rows = nc.dram_tensor("expert_rows", (E * CAP, D), F32, kind="Internal").ap()

        def sem(name):
            return ctx.enter_context(nc.semaphore(name))

        def sb(name, shape, dt=F32, c=ctx):
            return c.enter_context(nc.sbuf_tensor(name, shape, dt))

        banks = [ctx.enter_context(nc.psum_tensor(f"bank{i}", [P, 512], F32)) for i in range(8)]
        FFN2 = banks[4:8] + banks[3:4]
        SCORE, TURN = banks[0:2], banks[2:4]
        OUT, PROJ, QTURN, KTURN = banks[4], banks[5], banks[6], banks[7]

        x_sb = sb("x_sb", [P, TILES, D])
        identity = sb("identity", [P, P])
        stats = sb("stats", [P, TPB, 6])
        mean_var = sb("mean_var", [P, TPB, 2])
        var_eps = sb("var_eps", [P, TPB])
        std = sb("std", [P, TPB])
        rstd0 = sb("rstd0", [P, TPB])
        newton = sb("newton", [P, TPB])
        rstd = sb("rstd", [P, TPB])

        gate_sb = sb("gate_sb", [P, KC, E])
        xn2 = sb("xn2", [P, TPB, D])
        x2T = sb("x2T", [P, TPB * KC, P])
        before = sb("before", [P, P])
        ones = sb("ones", [P, P])
        iota8 = sb("iota8", [P, E])
        logit_max = sb("logit_max", [P, TPB])
        gates = sb("gates", [P, TPB, E])
        gate_sum = sb("gate_sum", [P, TPB])
        top_val = sb("top_val", [P, TPB, 8])
        top_idx = sb("top_idx", [P, TPB, 8], U32)
        top_e = sb("top_e", [P, TPB, TOPK])
        top_sum = sb("top_sum", [P, TPB])
        top_w = sb("top_w", [P, TPB, TOPK])
        onehot = sb("onehot", [P, TPB, TOPK, E])
        count = sb("count", [P, TPB, E])
        placed = sb("placed", [P, E])
        prefix = sb("prefix", [P, TPB, E])
        picked = sb("picked", [P, TPB, TOPK, E])
        position = sb("position", [P, TPB, TOPK])
        valid = sb("valid", [P, TPB, TOPK])
        slot_f = sb("slot_f", [P, TPB, TOPK])
        skip_f = sb("skip_f", [P, TPB, TOPK])
        scatter_idx = sb("scatter_idx", [P, TPB * TOPK], U32)
        gather_idx = sb("gather_idx", [P, TILES * TOPK], U32)
        item_w = sb("item_w", [P, TILES * TOPK])

        s_const = sem("s_const")
        s_x_in = [sem(f"s_x_in{b}") for b in range(B)]
        s_w0_in = sem("s_w0_in")
        s_wo_in = sem("s_wo_in")
        s_sink_in = sem("s_sink_in")
        s_weights_in = sem("s_weights_in")
        s_small_in = sem("s_small_in")
        s_gate_in = sem("s_gate_in")
        s_bias_in = sem("s_bias_in")
        s_rows_gone = sem("s_rows_gone")
        s_dve = sem("s_dve")
        s_pool = sem("s_pool")
        s_hi = sem("s_hi")
        s_pool2 = sem("s_pool2")
        s_ln = sem("s_ln")
        s_sink = sem("s_sink")
        s_denom = sem("s_denom")
        s_place = sem("s_place")
        s_route = sem("s_route")
        s_top = sem("s_top")
        s_first = sem("s_first")
        s_passed = sem("s_passed")
        s_var = sem("s_var")
        s_std = sem("s_std")
        s_norm = sem("s_norm")
        s_norm_turned = sem("s_norm_turned")
        s_xT = sem("s_xT")
        s_xcur = sem("s_xcur")
        s_proj = sem("s_proj")
        s_proj_out = sem("s_proj_out")
        s_v = sem("s_v")
        s_split = sem("s_split")
        s_qk_turned = sem("s_qk_turned")
        s_q_ready = sem("s_q_ready")
        s_k_ready = sem("s_k_ready")
        s_scores = sem("s_scores")
        s_neg_max = sem("s_neg_max")
        s_probs = sem("s_probs")
        s_turned = sem("s_turned")
        s_probs_t = [sem("s_probs_t_even"), sem("s_probs_t_odd")]
        s_sink_arg = sem("s_sink_arg")
        s_sink_exp = sem("s_sink_exp")
        s_recip = sem("s_recip")
        s_recip_wide = sem("s_recip_wide")
        s_recip_sb = sem("s_recip_sb")
        s_pv = sem("s_pv")
        s_heads = sem("s_heads")
        s_y = sem("s_y")
        s_residual = sem("s_residual")
        s_zero_rows = sem("s_zero_rows")
        s_norm2 = sem("s_norm2")
        s_norm2_turned = sem("s_norm2_turned")
        s_x2T = sem("s_x2T")
        s_logits = sem("s_logits")
        s_shifted = sem("s_shifted")
        s_gate_exp = sem("s_gate_exp")
        s_count = sem("s_count")
        s_prefix = sem("s_prefix")
        s_routed = sem("s_routed")
        s_scattered = sem("s_scattered")
        s_w1_in = sem("s_w1_in")
        s_w2_in = sem("s_w2_in")
        s_b1_turned = sem("s_b1_turned")
        s_b1 = sem("s_b1")
        s_w1_hi = sem("s_w1_hi")
        s_w1_lo = sem("s_w1_lo")
        s_w2_hi = sem("s_w2_hi")
        s_w2_lo = sem("s_w2_lo")
        s_slots_in = sem("s_slots_in")
        s_slots_turned = sem("s_slots_turned")
        s_slots_hi = sem("s_slots_hi")
        s_slots_lo = sem("s_slots_lo")
        s_hidden = sem("s_hidden")
        s_relu = sem("s_relu")
        s_hidden_hi = sem("s_hidden_hi")
        s_hidden_lo = sem("s_hidden_lo")
        s_expert = sem("s_expert")
        s_expert_sb = sem("s_expert_sb")
        s_expert_out = sem("s_expert_out")
        s_gathered = [sem("s_gathered0"), sem("s_gathered1")]
        s_combined = sem("s_combined")
        s_out = [sem("s_out0"), sem("s_out1")]

        actx = ExitStack()
        xT = sb("xT", [P, KC, T - L], c=actx)
        w_sb = sb("w_sb", [P, KC, NKV, GW], c=actx)
        wo_sb = sb("wo_sb", [P, NQ // 2, D], c=actx)
        xcur = sb("xcur", [P, KC, L], c=actx)
        xn = sb("xn", [P, 2, D], c=actx)
        zeros = sb("zeros", [P, D], c=actx)
        mask = sb("mask", [P, TPB, L], c=actx)
        rope_sb = sb("rope_sb", [P, TPB, 3, RH], c=actx)
        identity_r = sb("identity_r", [P, P], F32R, c=actx)
        sink_all = sb("sink_all", [P, NQ], c=actx)
        sink_cur = sb("sink_cur", [P, 2, QM], c=actx)
        sink_neg = sb("sink_neg", [P, 2, QM], c=actx)
        qk_sb = [sb(f"qk_sb{i}", [P, GW - HD], c=actx) for i in range(2)]
        v_next = sb("v_next", [P, TPB, HD], c=actx)
        rot_a = sb("rot_a", [P, (QM + 1) * 2 * RH], c=actx)
        rot_b = sb("rot_b", [P, (QM + 1) * 2 * RH], c=actx)
        qk_split = [sb(f"qk_split{i}", [P, 6 * P], F32R, c=actx) for i in range(2)]
        q_st = [sb(f"q_st{i}", [P, QM, L], F32R, c=actx) for i in range(2)]
        k_st = [sb(f"k_st{i}", [P, 2, L], F32R, c=actx) for i in range(2)]
        v_sb = [sb(f"v_sb{i}", [P, TPB, HD], c=actx) for i in range(2)]
        probs = [sb(f"probs{i}", [P, L], c=actx) for i in range(RING)]
        probs_t = [sb(f"probs_t{h}", [P, TPB, L], c=actx) for h in range(QM)]
        neg_max = [sb(f"neg_max{i}", [P, UNITS], c=actx) for i in range(2)]
        sums = [sb(f"sums{i}", [P, UNITS], c=actx) for i in range(2)]
        sink_arg = sb("sink_arg", [P, UNITS], c=actx)
        sink_exp = sb("sink_exp", [P, UNITS], c=actx)
        denom = sb("denom", [P, UNITS], c=actx)
        recip = sb("recip", [P, UNITS], c=actx)
        recip_cols = sb("recip_cols", [P, TPB, 2, HD], c=actx)
        recip_sb = [sb(f"recip_sb{p}", [P, L], c=actx) for p in range(PAIRS)]
        heads = [sb(f"heads{p}", [P, L], c=actx) for p in range(PAIRS)]
        actx.close()

        mctx = ExitStack()
        w1_raw = sb("w1_raw", [P, KC, HID], c=mctx)
        w2_raw = sb("w2_raw", [P, HC, D], c=mctx)
        b1_rows = sb("b1_rows", [E * HC, P], c=mctx)
        b1_sb = sb("b1_sb", [P, E, HC], c=mctx)
        b1_cur = sb("b1_cur", [P, HC], c=mctx)
        b2_sb = sb("b2_sb", [P, E, D], c=mctx)
        w1_hi = sb("w1_hi", [P, KC, HID], F32R, c=mctx)
        w1_lo = sb("w1_lo", [P, KC, HID], F32R, c=mctx)
        w2_hi = sb("w2_hi", [P, HC, D], F32R, c=mctx)
        w2_lo = sb("w2_lo", [P, HC, D], F32R, c=mctx)
        slots = sb("slots", [P, SLOTT, D], c=mctx)
        slots_hi = sb("slots_hi", [P, KC * CAP], F32R, c=mctx)
        slots_lo = sb("slots_lo", [P, KC * CAP], F32R, c=mctx)
        hidden = [sb(f"hidden{i}", [P, CAP], c=mctx) for i in range(2)]
        hidden_hi = sb("hidden_hi", [P, HC, CAP], F32R, c=mctx)
        hidden_lo = sb("hidden_lo", [P, HC, CAP], F32R, c=mctx)
        expert_sb = sb("expert_sb", [P, SLOTT, D], c=mctx)
        gathered = [sb(f"gathered{i}", [P, TPB * TOPK, D], c=mctx) for i in range(2)]
        combined = [sb(f"combined{i}", [P, TPB, D], c=mctx) for i in range(2)]
        mctx.close()

        AHEAD = {
            "pe": [s_pv, s_y],
            "pool": [s_rows_gone],
            "dve": [s_heads, s_residual],
        }

        def start_ahead(eng, name):
            for s in AHEAD[name]:
                eng.sem_inc(s, 1)

        def later(n):
            return not isinstance(n, int) or n > 0

        def plain(eng):
            eng.sem_inc(s_passed, 1)

        x_rows = x.rearrange("b (t p) d -> p (b t) d", p=P)
        out_rows = out.rearrange("b (t p) d -> p (b t) d", p=P)

        PROJ_AT = {-15: 0, -13: 1, -12: 2, -7: 3}
        QK_AT = {-11: 0, -8: 1, -5: 2, -2: 3}
        PV_AT = {13 + 8 * p + c: (p, c) for p in range(PAIRS) for c in range(TPB)}
        SINK_AT = {8: 0, 16: 1}
        RECIP_AT = {10: 0, 17: 1}
        WIDEN_AT = {13: 0, 19: 1}
        HEADS_AT = {17: 0, 25: 1}
        Y_AT = {26: 0, 28: 1}

        def period(step, g, j, prev=True, cur=True, nxt=True, also=None, b=None):
            for n in range(UNITS):
                if cur:
                    step(n, g, j, int(nxt), b)
                if prev:
                    step(n + UNITS, g - 1, 1 - j, int(cur) + int(nxt), None)
                if nxt:
                    step(n - UNITS, g + 1, 1 - j, 2, b)
                if also:
                    also(n)

        ROUTE_FROM = -4

        def all_periods(eng, step, route):
            def route_first(b):
                return lambda n: route(n - UNITS, b, False) if n - UNITS >= ROUTE_FROM else None

            period(step, 0, 0, prev=False)
            period(step, 1, 1)
            with eng.Fori(0, B - 1) as b:
                with eng.Fori(0, NKV // 2 - 1) as i:
                    for k in range(2):
                        period(step, b * NKV + i * 2 + (k + 2), k)
                period(step, b * NKV + NKV, 0, also=route_first(b))
                period(step, b * NKV + (NKV + 1), 1, also=lambda n: route(n, b, False), b=b)
            with eng.Fori(0, NKV // 2 - 2) as i:
                for k in range(2):
                    period(step, i * 2 + (GROUPS - NKV + 2 + k), k)
            period(step, GROUPS - 2, 0)
            period(step, GROUPS - 1, 1, nxt=False)
            period(step, GROUPS, 0, cur=False, nxt=False, also=route_first(B - 1))
            for r in range(UNITS):
                route(r, B - 1, True)

        block = ctx.enter_context(nc.Block())

        @block.sync
        def _(sp):
            sp.dma_start(x_sb[:, 0:TPB, :], x_rows[:, 0:TPB, :]).then_inc(s_x_in[0], 16)
            QW, KW = NQ * HD, NKV * HD
            parts = [(0, QM * HD, 0), (QM * HD, HD, QW), (QM * HD + HD, HD, QW + KW)]
            for at, width, col in parts:
                sp.dma_start(w_sb[:, :, 0, at:at + width],
                             w_qkv[:, col:col + width].rearrange("(c p) n -> p c n", p=P)).then_inc(s_w0_in, 16)
            sp.dma_start(rope_sb[:, :, :, :], rope).then_inc(s_small_in, 16)
            sp.wait_ge(s_w0_in, 16 * 3)
            for b in range(1, B):
                sp.dma_start(x_sb[:, b * TPB:(b + 1) * TPB, :],
                             x_rows[:, b * TPB:(b + 1) * TPB, :]).then_inc(s_x_in[b], 16)
            for kc in range(KC):
                rows = w_qkv[kc * P:(kc + 1) * P, :]
                for at, width, col in parts:
                    sp.dma_start(w_sb[:, kc, 1:NKV, at:at + width],
                                 rows[:, col + width:col + NKV * width].rearrange("p (g n) -> p g n", n=width)
                                 ).then_inc(s_weights_in, 16)
            sp.dma_start(sink_all[:, :], sink.rearrange("a k m -> a (k m)").partition_broadcast(P)
                         .rearrange("p a n -> p (a n)")).then_inc(s_sink_in, 16)
            sp.dma_start(wo_sb[:, :, :], w_out.rearrange("(c p) n -> p c n", p=P)).then_inc(s_wo_in, 16)
            sp.dma_start(gate_sb[:, :, :], gate_w.rearrange("(c p) e -> p c e", p=P)).then_inc(s_gate_in, 16)
            sp.wait_ge(s_xT, TPB)
            sp.sem_inc(s_xcur, 16)
            sp.wait_ge(s_const, 3)
            sp.dma_start(slot_rows.rearrange("(p j) d -> p j d", p=P),
                         zeros[:, :].unsqueeze(1).broadcast_to([P, E * CAP // P, D])).then_inc(s_zero_rows, 16)
            sp.wait_ge(s_xT, TILES)
            with sp.Fori(1, B) as b:
                sp.wait_ge(s_proj, b * (NKV * TPB))
                sp.dma_start(xcur[:, :, :], xT[:, :, bass.ds(b * L - L, L)]).then_inc(s_xcur, 16)
            sp.wait_ge(s_xcur, 16 * B)
            sp.wait_ge(s_proj, GROUPS * TPB)
            sp.dma_start(w1_raw[:, :, :], w1[0].rearrange("(c p) n -> p c n", p=P)).then_inc(s_w1_in, 16)
            sp.dma_start(w2_raw[:, :, :], w2[0].rearrange("(c p) n -> p c n", p=P)).then_inc(s_w2_in, 16)
            sp.wait_ge(s_residual, 2 * GROUPS + 1)
            sp.dma_start(b1_rows[:, :], b1.rearrange("e (c p) -> (e c) p", p=P)).then_inc(s_bias_in, 16)
            sp.dma_start(b2_sb[:, :, :].rearrange("p e d -> p (e d)"),
                         b2.rearrange("(a e) d -> a (e d)", a=1).partition_broadcast(P)
                         .rearrange("p a n -> p (a n)")).then_inc(s_bias_in, 16)
            sp.wait_ge(s_scattered, 16 * TILES * TOPK)
            def slots_in(e):
                sp.dma_start(slots[:, :, :], slot_rows[bass.ds(e * CAP, CAP), :]
                             .rearrange("(p j) d -> p j d", j=SLOTT)).then_inc(s_slots_in, 16)

            def rows_out(e):
                sp.wait_ge(s_expert_sb, SLOTT * e + SLOTT)
                sp.dma_start(expert_rows[bass.ds(e * CAP, CAP), :].rearrange("(p j) d -> p j d", j=SLOTT),
                             expert_sb[:, :, :]).then_inc(s_expert_out, 16)

            slots_in(0)
            with sp.Fori(0, E - 1) as e:
                sp.wait_ge(s_slots_turned, e * 3 + 3)
                slots_in(e + 1)
                sp.wait_ge(s_w1_hi, e + 1)
                sp.wait_ge(s_w1_lo, e + 1)
                sp.dma_start(w1_raw[:, :, :], w1[bass.ds(e + 1, 1)].rearrange("a (c p) n -> p (a c) n", p=P)
                             ).then_inc(s_w1_in, 16)
                sp.wait_ge(s_w2_hi, e + 1)
                sp.wait_ge(s_w2_lo, e + 1)
                sp.dma_start(w2_raw[:, :, :], w2[bass.ds(e + 1, 1)].rearrange("a (c p) n -> p (a c) n", p=P)
                             ).then_inc(s_w2_in, 16)
                rows_out(e)
            rows_out(E - 1)
            with sp.Fori(0, B // 2) as half:
                for i in range(2):
                    sp.wait_ge(s_combined, half * 2 + i + 1)
                    sp.dma_start(out_rows[:, bass.ds((half * 2 + i) * TPB, TPB), :],
                                 combined[i][:, :, :]).then_inc(s_out[i], 16)
            for i in range(2):
                sp.wait_ge(s_out[i], 16 * (B // 2))

        @block.gpsimd
        def _(pool):
            start_ahead(pool, "pool")
            steps = [0]

            def own(ins):
                steps[0] += 1
                ins.then_inc(s_pool, 1)
                pool.wait_ge(s_pool, steps[0])

            own(nc.gpsimd.memset(identity[:, :], 0.0))
            nc.gpsimd.affine_select(out=identity[:, :], in_=identity[:, :], compare_op=ALU.not_equal, fill=1.0,
                                    base=0, pattern=[[-1, P]], channel_multiplier=1).then_inc(s_const, 1)
            pool.wait_ge(s_const, 1)
            nc.gpsimd.tensor_copy(identity_r[:, :], identity[:, :]).then_inc(s_const, 1)
            nc.gpsimd.memset(zeros[:, :], 0.0)
            own(nc.gpsimd.memset(mask[:, :, :], MASKED))
            for t in range(TPB):
                own(nc.gpsimd.affine_select(out=mask[:, t, :], in_=mask[:, t, :], compare_op=ALU.is_ge, fill=0.0,
                                            base=t * P, pattern=[[-1, L]], channel_multiplier=1))
                last = nc.gpsimd.affine_select(out=mask[:, t, :], in_=mask[:, t, :], compare_op=ALU.is_ge, fill=0.0,
                                               base=BAND - 1 - t * P, pattern=[[1, L]], channel_multiplier=-1)
                if t < TPB - 1:
                    own(last)
            last.then_inc(s_const, 1)
            before_group = steps[0]
            ROT_STEPS = 4

            def split(g, t):
                q = g * TPB + t
                pool.wait_ge(s_proj_out, q + 1)
                if later(q - 1):
                    pool.wait_ge(s_qk_turned, q - 1)
                src, dst = qk_sb[t % 2], qk_split[t % 2]
                NH = QM + 1
                rot = src[:, :].rearrange("p (h j r) -> p h j r", j=2, r=HD // 2)[:, :, :, 0:RH]
                cos = rope_sb[:, t, 0, :].unsqueeze(1).unsqueeze(1)
                sin = rope_sb[:, t, 1, :].unsqueeze(1)
                nsin = rope_sb[:, t, 2, :].unsqueeze(1)
                a = rot_a[:, :].rearrange("p (h j r) -> p h j r", j=2, r=RH)
                c = rot_b[:, :].rearrange("p (h j r) -> p h j r", j=2, r=RH)
                base = before_group + q * ROT_STEPS
                nc.gpsimd.tensor_tensor(a, rot, cos.broadcast_to([P, NH, 2, RH]), ALU.mult).then_inc(s_pool, 1)
                nc.gpsimd.tensor_tensor(c[:, :, 0, :], rot[:, :, 1, :], sin.broadcast_to([P, NH, RH]),
                                        ALU.mult).then_inc(s_pool, 1)
                nc.gpsimd.tensor_tensor(c[:, :, 1, :], rot[:, :, 0, :], nsin.broadcast_to([P, NH, RH]),
                                        ALU.mult).then_inc(s_pool, 1)
                pool.wait_ge(s_pool, base + 3)
                nc.gpsimd.tensor_tensor(rot, a, c, ALU.add).then_inc(s_pool, 1)
                pool.wait_ge(s_pool, base + 4)
                plain(pool)
                q_in = src[:, 0:QM * HD].rearrange("p (h d) -> p h d", d=HD)
                k_in = src[:, QM * HD:NH * HD].unsqueeze(1).broadcast_to([P, 2, HD])
                q_out = dst[:, 0:QM * P].rearrange("p (h s d) -> p h s d", s=2, d=HD)
                k_hi = dst[:, QM * P:(QM + 1) * P].rearrange("p (s d) -> p s d", d=HD)
                k_lo = dst[:, (QM + 1) * P:(QM + 2) * P].rearrange("p (s d) -> p s d", d=HD)
                nc.gpsimd.tensor_copy(q_out[:, :, 0, :], q_in)
                nc.gpsimd.tensor_copy(k_hi, k_in).then_inc(s_hi, 1)
                pool.wait_ge(s_hi, q + 1)
                nc.gpsimd.tensor_tensor(q_out[:, :, 1, :], q_in, q_out[:, :, 0, :].bitcast(F32), ALU.subtract)
                nc.gpsimd.tensor_tensor(k_lo, k_in, k_hi.bitcast(F32), ALU.subtract).then_inc(s_split, 1)

            def keep_v(g, j):
                if later(2 * g - 2):
                    pool.wait_ge(s_pv, 2 * g - 2 + 1)
                plain(pool)
                nc.gpsimd.tensor_copy(v_sb[j][:, :, :], v_next[:, :, :]).then_inc(s_v, 1)

            pool.wait_ge(s_small_in, 16)
            def group(g, j, routed=None):
                for t in range(TPB):
                    split(g, t)
                    if routed is not None:
                        scatter(routed, t)
                keep_v(g, j)

            def scatter(b, t):
                if t == 0:
                    pool.wait_ge(s_routed, b + 1)
                plain(pool)
                for k in range(TOPK):
                    c = t * TOPK + k
                    nc.gpsimd.indirect_dma_start(
                        slot_rows, bass.IndirectOffsetOnAxis(ap=scatter_idx[:, c:c + 1], axis=0),
                        xn2[:, t, :], None, bounds_check=E * CAP - 1, oob_is_err=False).then_inc(s_scattered, 16)

            group(0, 0)
            nc.gpsimd.memset(ones[:, :], 1.0)
            nc.gpsimd.iota(iota8[:, :], pattern=[[1, E]], base=0, channel_multiplier=0,
                           allow_small_or_imprecise_dtypes=True)
            nc.gpsimd.memset(before[:, :], 1.0).then_inc(s_pool2, 1)
            pool.wait_ge(s_pool2, 1)
            nc.gpsimd.affine_select(out=before[:, :], in_=before[:, :], compare_op=ALU.is_gt, fill=0.0, base=0,
                                    pattern=[[1, P]], channel_multiplier=-1).then_inc(s_const, 1)
            for g in range(1, 4):
                group(g, g % 2)
            pool.wait_ge(s_zero_rows, 16)
            with pool.Fori(0, B - 1) as b:
                with pool.Fori(0, NKV // 2 - 1) as i:
                    for j in range(2):
                        group(b * NKV + i * 2 + (j + 4), j)
                group(b * NKV + (NKV + 2), 0)
                group(b * NKV + (NKV + 3), 1, routed=b)
                pool.wait_ge(s_scattered, b * (16 * TPB * TOPK) + 16 * TPB * TOPK)
                pool.sem_inc(s_rows_gone, 1)
            with pool.Fori(0, NKV // 2 - 2) as i:
                for j in range(2):
                    group(i * 2 + (GROUPS - NKV + 4 + j), j)
            for t in range(TPB):
                scatter(B - 1, t)
            with pool.Fori(0, E) as e:
                pool.wait_ge(s_w1_hi, e + 1)
                nc.gpsimd.tensor_tensor(w1_lo[:, :, :], w1_raw[:, :, :], w1_hi[:, :, :].bitcast(F32),
                                        ALU.subtract).then_inc(s_w1_lo, 1)
                pool.wait_ge(s_w2_hi, e + 1)
                nc.gpsimd.tensor_tensor(w2_lo[:, :, :], w2_raw[:, :, :], w2_hi[:, :, :].bitcast(F32),
                                        ALU.subtract).then_inc(s_w2_lo, 1)
            pool.wait_ge(s_expert_out, 16 * E)
            for b in range(B):
                if later(b - 1):
                    pool.wait_ge(s_combined, b - 1)
                for c in range(TPB * TOPK):
                    n = b * TPB * TOPK + c
                    nc.gpsimd.indirect_dma_start(
                        gathered[b % 2][:, c, :], None, expert_rows,
                        bass.IndirectOffsetOnAxis(ap=gather_idx[:, n:n + 1], axis=0)).then_inc(s_gathered[b % 2], 16)

        @block.scalar
        def _(act):
            def norm_out(b):
                act.wait_ge(s_var, b + 1)
                nc.scalar.activation(std[:, :], var_eps[:, :], ACT.Sqrt).then_inc(s_std, 1)
                for t in range(TPB):
                    act.wait_ge(s_norm_turned, b * TPB + t + 1)
                    rows = xcur[:, :, t * P:(t + 1) * P] if b == 0 else xT[:, :, (b - 1) * L + t * P:(b - 1) * L + (t + 1) * P]
                    nc.scalar.activation(rows,
                                         SCORE[t % 2][:, 0:D].rearrange("p (c q) -> p c q", c=KC),
                                         ACT.Copy).then_inc(s_xT, 1)

            def proj_out(g, t):
                q = g * TPB + t
                act.wait_ge(s_proj, q + 1)
                if later(q - 1):
                    act.wait_ge(s_split, q - 1)
                if t == 0 and later(g):
                    act.wait_ge(s_v, g)
                nc.scalar.activation(qk_sb[t % 2][:, :], PROJ[:, 0:GW - HD], ACT.Copy)
                nc.scalar.activation(v_next[:, t, :], PROJ[:, GW - HD:GW], ACT.Copy).then_inc(s_proj_out, 1)

            def k_out(g, j, t):
                act.wait_ge(s_qk_turned, g * TPB + t + 1)
                nc.scalar.activation(k_st[j][:, :, t * P:(t + 1) * P],
                                     KTURN[:, 0:2 * P].rearrange("p (s q) -> p s q", s=2),
                                     ACT.Copy).then_inc(s_k_ready, 1)

            def act_step(n, g, j, follow, routed):
                if n in PROJ_AT:
                    proj_out(g, PROJ_AT[n])
                if n in QK_AT:
                    k_out(g, j, QK_AT[n])
                if n - 1 in WIDEN_AT:
                    p = WIDEN_AT[n - 1]
                    act.wait_ge(s_recip_wide, 2 * g + p + 1)
                    if later(2 * g + p - 1):
                        act.wait_ge(s_heads, 2 * g + p - 1 + 1)
                    nc.scalar.activation(recip_sb[p][:, :], QTURN[:, :], ACT.Copy).then_inc(s_recip_sb, 1)
                if 0 <= n < UNITS:
                    act.wait_ge(s_neg_max, g * UNITS + n + 1)
                    nc.scalar.activation(probs[n % RING][:, :], probs[n % RING][:, :], ACT.Exp,
                                         bias=neg_max[j][:, n:n + 1], scale=-1.0,
                                         accum_out=sums[j][:, n:n + 1]).then_inc(s_probs, 1)
                u = n - LAG
                if 0 <= u < UNITS and u % 2 == 1:
                    h, t = divmod(u, TPB)
                    act.wait_ge(s_turned, g * UNITS + u + 1)
                    if later(2 * g - 1 + h // 2):
                        act.wait_ge(s_pv, 2 * g - 1 + h // 2 + 1)
                    nc.scalar.activation(probs_t[h][:, :, t * P:(t + 1) * P],
                                         TURN[1][:, :].rearrange("p (c q) -> p c q", c=TPB),
                                         ACT.Copy).then_inc(s_probs_t[1], 1)
                if n in SINK_AT:
                    p = SINK_AT[n]
                    act.wait_ge(s_sink_arg, 2 * g + p + 1)
                    nc.scalar.activation(sink_exp[:, 8 * p:8 * p + 8], sink_arg[:, 8 * p:8 * p + 8],
                                         ACT.Exp).then_inc(s_sink_exp, 1)

            norm_out(0)
            proj_out(0, 0)
            proj_out(0, 1)
            norm_out(1)
            proj_out(0, 2)
            k_out(0, 0, 0)
            norm_out(2)
            proj_out(0, 3)
            k_out(0, 0, 1)
            norm_out(3)
            k_out(0, 0, 2)
            k_out(0, 0, 3)
            def act_route(r, b, last):
                if r == 0:
                    act.wait_ge(s_var, b + (B + 1))
                    nc.scalar.activation(std[:, :], var_eps[:, :], ACT.Sqrt).then_inc(s_std, 1)
                if r in (3, 4):
                    half = r - 3
                    act.wait_ge(s_norm2_turned, b * 2 + half + 1)
                    nc.scalar.activation(x2T[:, half * 4:half * 4 + 4, :],
                                         KTURN[:, :].rearrange("p (c q) -> p c q", c=4),
                                         ACT.Copy).then_inc(s_x2T, 1)
                if r == 7:
                    act.wait_ge(s_shifted, b + 1)
                    nc.scalar.activation(gates[:, :, :], gates[:, :, :], ACT.Exp).then_inc(s_gate_exp, 1)

            all_periods(act, act_step, act_route)
            act.wait_ge(s_residual, 2 * GROUPS + 1)
            act.wait_ge(s_b1_turned, 1)
            nc.scalar.activation(b1_sb[:, :, :], PROJ[:, 0:E * HC].rearrange("p (e c) -> p e c", e=E),
                                 ACT.Copy).then_inc(s_b1, 1)
            act.wait_ge(s_b1, 1)

            def w1_split(e):
                act.wait_ge(s_w1_in, e * 16 + 16)
                if later(e):
                    act.wait_ge(s_hidden, e * HC)
                nc.scalar.activation(w1_hi[:, :, :], w1_raw[:, :, :], ACT.Copy).then_inc(s_w1_hi, 1)
                if later(e):
                    act.wait_ge(s_relu, e * HC)
                nc.scalar.activation(b1_cur[:, :], b1_sb[:, bass.ds(e, 1), :].rearrange("p a c -> p (a c)"),
                                     ACT.Copy).then_inc(s_b1, 1)

            def w2_split(e):
                act.wait_ge(s_w2_in, e * 16 + 16)
                if later(e):
                    act.wait_ge(s_expert, e * SLOTT)
                nc.scalar.activation(w2_hi[:, :, :], w2_raw[:, :, :], ACT.Copy).then_inc(s_w2_hi, 1)

            def slots_split(e):
                for c in range(3):
                    act.wait_ge(s_slots_turned, e * 3 + (c + 1))
                    n0, n1 = c * 512, min(KC * CAP, c * 512 + 512)
                    nc.scalar.activation(slots_hi[:, n0:n1], banks[c][:, 0:n1 - n0],
                                         ACT.Copy).then_inc(s_slots_hi, 1)

            def relus(e, with_w2):
                act.wait_ge(s_b1, e + 2)
                for c in range(HC):
                    n = e * HC + c
                    act.wait_ge(s_hidden, n + 1)
                    if later(n - 1):
                        act.wait_ge(s_hidden_lo, n - 1)
                    for half in range(2):
                        ins = nc.scalar.activation(hidden[c % 2][:, half * HALF:(half + 1) * HALF],
                                                   banks[4 + 2 * (c % 2) + half][:, 0:HALF], ACT.Relu,
                                                   bias=b1_cur[:, c:c + 1])
                    ins.then_inc(s_relu, 1)
                    if c == 1 and with_w2:
                        w2_split(e)

            w1_split(0)
            w2_split(0)
            slots_split(0)
            relus(0, False)
            with act.Fori(1, E) as e:
                slots_split(e)
                w1_split(e)
                relus(e, True)

        @block.vector
        def _(dve):
            start_ahead(dve, "dve")
            def layernorm_stats(src, n):
                k = n * 13
                for t in range(TPB):
                    nc.vector.bn_stats(stats[:, t, :], src(t)).then_inc(s_ln, 1)
                    dve.wait_ge(s_ln, k + 2 * t + 1)
                    plain(dve)
                    nc.vector.bn_aggr(mean_var[:, t, :], stats[:, t, :]).then_inc(s_ln, 1)
                dve.wait_ge(s_ln, k + 8)
                nc.vector.tensor_scalar(var_eps[:, :], mean_var[:, :, 1], EPS, None, ALU.add).then_inc(s_var, 1)
                dve.wait_ge(s_std, n + 1)
                nc.vector.reciprocal(rstd0[:, :], std[:, :]).then_inc(s_ln, 1)
                dve.wait_ge(s_ln, k + 9)
                nc.vector.tensor_tensor(newton[:, :], rstd0[:, :], rstd0[:, :], ALU.mult).then_inc(s_ln, 1)
                dve.wait_ge(s_ln, k + 10)
                nc.vector.tensor_tensor(newton[:, :], newton[:, :], var_eps[:, :], ALU.mult).then_inc(s_ln, 1)
                dve.wait_ge(s_ln, k + 11)
                nc.vector.tensor_scalar(newton[:, :], newton[:, :], -0.5, 1.5, ALU.mult, ALU.add).then_inc(s_ln, 1)
                dve.wait_ge(s_ln, k + 12)
                nc.vector.tensor_tensor(rstd[:, :], rstd0[:, :], newton[:, :], ALU.mult).then_inc(s_ln, 1)
                dve.wait_ge(s_ln, k + 13)

            nc.vector.memset(placed[:, :], 0.0).then_inc(s_place, 1)
            def norm(b):
                dve.wait_ge(s_x_in[b], 16)
                layernorm_stats(lambda t: x_sb[:, b * TPB + t, :], b)
                for t in range(TPB):
                    if later(b * TPB + t - 1):
                        dve.wait_ge(s_norm_turned, b * TPB + t - 1)
                    nc.vector.tensor_scalar(xn[:, t % 2, :], x_sb[:, b * TPB + t, :], mean_var[:, t, 0:1],
                                            rstd[:, t:t + 1], ALU.subtract, ALU.mult).then_inc(s_norm, 1)

            def q_out(g, j, t):
                dve.wait_ge(s_qk_turned, g * TPB + t + 1)
                nc.vector.tensor_copy(q_st[j][:, :, t * P:(t + 1) * P],
                                      QTURN[:, :].rearrange("p (h q) -> p h q", h=QM)).then_inc(s_q_ready, 1)

            def sinks(g, j):
                cols = sink_all[:, bass.ds((g % NKV) * QM, QM)]
                nc.vector.tensor_copy(sink_cur[:, j, :], cols).then_inc(s_sink, 1)
                nc.vector.tensor_scalar(sink_neg[:, j, :], cols, -1.0, None, ALU.mult).then_inc(s_sink, 1)

            def dve_step(n, g, j, follow, routed):
                if n == -1:
                    sinks(g, j)
                if 0 <= n < UNITS:
                    U = g * UNITS + n
                    h, t = divmod(n, TPB)
                    dve.wait_ge(s_scores, U + 1)
                    if n == 0:
                        dve.wait_ge(s_sink, 2 * g + 2)
                    if later(U - RING + 1):
                        dve.wait_ge(s_turned, U - RING + 1)
                    plain(dve)
                    nc.vector.tensor_tensor_reduce(
                        probs[n % RING][:, :], SCORE[n % 2][:, :], mask[:, t, :], -SCALE, sink_neg[:, j, h:h + 1],
                        ALU.add, ALU.min, neg_max[j][:, n:n + 1]).then_inc(s_neg_max, 1)
                u = n - LAG
                if 0 <= u < UNITS and u % 2 == 0:
                    h, t = divmod(u, TPB)
                    dve.wait_ge(s_turned, g * UNITS + u + 1)
                    if later(2 * g - 1 + h // 2):
                        dve.wait_ge(s_pv, 2 * g - 1 + h // 2 + 1)
                    nc.vector.tensor_copy(probs_t[h][:, :, t * P:(t + 1) * P],
                                          TURN[0][:, :].rearrange("p (c q) -> p c q", c=TPB)
                                          ).then_inc(s_probs_t[0], 1)
                if n in SINK_AT:
                    p = SINK_AT[n]
                    dve.wait_ge(s_neg_max, g * UNITS + 8 * p + 8)
                    nc.vector.tensor_tensor(
                        sink_arg[:, 8 * p:8 * p + 8].rearrange("p (h t) -> p h t", t=TPB),
                        neg_max[j][:, 8 * p:8 * p + 8].rearrange("p (h t) -> p h t", t=TPB),
                        sink_cur[:, j, 2 * p:2 * p + 2].unsqueeze(2).broadcast_to([P, 2, TPB]),
                        ALU.add).then_inc(s_sink_arg, 1)
                if n in RECIP_AT:
                    p = RECIP_AT[n]
                    dve.wait_ge(s_probs, g * UNITS + 8 * p + 8)
                    dve.wait_ge(s_sink_exp, 2 * g + p + 1)
                    nc.vector.tensor_tensor(denom[:, 8 * p:8 * p + 8], sums[j][:, 8 * p:8 * p + 8],
                                            sink_exp[:, 8 * p:8 * p + 8], ALU.add).then_inc(s_denom, 1)
                    dve.wait_ge(s_denom, 4 * g + 2 * p + 1)
                    nc.vector.reciprocal(recip[:, 8 * p:8 * p + 8], denom[:, 8 * p:8 * p + 8]).then_inc(s_denom, 1)
                    dve.wait_ge(s_denom, 4 * g + 2 * p + 2)
                    if later(2 * g + p):
                        dve.wait_ge(s_recip_wide, 2 * g + p)
                    nc.vector.tensor_copy(recip_cols[:, :, :, :],
                                          recip[:, 8 * p:8 * p + 8].rearrange("p (h t) -> p t h", t=TPB)
                                          .unsqueeze(3).broadcast_to([P, TPB, 2, HD])).then_inc(s_recip, 1)
                if n in HEADS_AT:
                    p = HEADS_AT[n]
                    dve.wait_ge(s_pv, 2 * g + p + 1 + 1)
                    dve.wait_ge(s_recip_sb, 2 * g + p + 1)
                    if later(2 * g):
                        dve.wait_ge(s_y, 2 * g + 1)
                    nc.vector.tensor_tensor(heads[p][:, :], OUT[:, :], recip_sb[p][:, :], ALU.mult).then_inc(s_heads, 1)
                if n - 1 in Y_AT:
                    half = Y_AT[n - 1]
                    dve.wait_ge(s_y, 2 * g + half + 1 + 1)
                    if later(2 * g):
                        dve.wait_ge(s_residual, 2 * g + 1)
                    rows = x_sb[:, bass.ds((g // NKV) * TPB + 2 * half, 2), :]
                    nc.vector.tensor_tensor(rows, rows, PROJ[:, :].rearrange("p (t d) -> p t d", t=2),
                                            ALU.add).then_inc(s_residual, 1)
                if n in QK_AT:
                    q_out(g, j, QK_AT[n])

            norm(0)
            norm(1)
            q_out(0, 0, 0)
            norm(2)
            q_out(0, 0, 1)
            norm(3)
            q_out(0, 0, 2)
            q_out(0, 0, 3)
            dve.wait_ge(s_sink_in, 16)
            sinks(0, 0)
            def dve_route(r, b, last):
                def step(ins, n):
                    ins.then_inc(s_route, 1)
                    dve.wait_ge(s_route, b * 12 + n)

                def ln(ins, n):
                    ins.then_inc(s_ln, 1)
                    dve.wait_ge(s_ln, (b + B) * 13 + n)

                if r < 0:
                    t = r - ROUTE_FROM
                    dve.wait_ge(s_residual, b * (2 * NKV) + (2 * NKV + t // 2))
                    plain(dve)
                    ln(nc.vector.bn_stats(stats[:, t, :], x_sb[:, bass.ds(b * TPB + t, 1), :]
                                          .rearrange("p a d -> p (a d)")), 2 * t + 1)
                    plain(dve)
                    nc.vector.bn_aggr(mean_var[:, t, :], stats[:, t, :]).then_inc(s_ln, 1)
                if r == 0:
                    dve.wait_ge(s_ln, (b + B) * 13 + 8)
                    nc.vector.tensor_scalar(var_eps[:, :], mean_var[:, :, 1], EPS, None, ALU.add).then_inc(s_var, 1)
                if r == 1:
                    dve.wait_ge(s_std, b + (B + 1))
                    ln(nc.vector.reciprocal(rstd0[:, :], std[:, :]), 9)
                    ln(nc.vector.tensor_tensor(newton[:, :], rstd0[:, :], rstd0[:, :], ALU.mult), 10)
                    ln(nc.vector.tensor_tensor(newton[:, :], newton[:, :], var_eps[:, :], ALU.mult), 11)
                if r == 2:
                    ln(nc.vector.tensor_scalar(newton[:, :], newton[:, :], -0.5, 1.5, ALU.mult, ALU.add), 12)
                    ln(nc.vector.tensor_tensor(rstd[:, :], rstd0[:, :], newton[:, :], ALU.mult), 13)
                    dve.wait_ge(s_rows_gone, b + 1)
                if r in (2, 3):
                    for t in (2 * r - 4, 2 * r - 3):
                        nc.vector.tensor_scalar(xn2[:, t, :],
                                                x_sb[:, bass.ds(b * TPB + t, 1), :].rearrange("p a d -> p (a d)"),
                                                mean_var[:, t, 0:1], rstd[:, t:t + 1],
                                                ALU.subtract, ALU.mult).then_inc(s_norm2, 1)
                if r == 7:
                    dve.wait_ge(s_logits, b + 1)
                    logits = PROJ[:, 0:TPB * E].rearrange("p (t e) -> p t e", e=E)
                    step(nc.vector.tensor_reduce(logit_max[:, :], logits, AX, ALU.max), 1)
                    nc.vector.tensor_tensor(gates[:, :, :], logits,
                                            logit_max[:, :].unsqueeze(2).broadcast_to([P, TPB, E]),
                                            ALU.subtract).then_inc(s_shifted, 1)
                if r == 8:
                    dve.wait_ge(s_gate_exp, b + 1)
                    step(nc.vector.tensor_reduce(gate_sum[:, :], gates[:, :, :], AX, ALU.add), 2)
                    step(nc.vector.reciprocal(gate_sum[:, :], gate_sum[:, :]), 3)
                    step(nc.vector.tensor_tensor(gates[:, :, :], gates[:, :, :],
                                                 gate_sum[:, :].unsqueeze(2).broadcast_to([P, TPB, E]), ALU.mult), 4)
                if r == 9:
                    plain(dve)
                    for t in range(TPB):
                        nc.vector.max(top_val[:, t, :], gates[:, t, :]).then_inc(s_top, 1)
                    dve.wait_ge(s_top, b * (2 * TPB) + TPB)
                    plain(dve)
                    for t in range(TPB):
                        nc.vector.max_index(top_idx[:, t, :], top_val[:, t, :], gates[:, t, :]).then_inc(s_top, 1)
                if r == 10:
                    dve.wait_ge(s_top, b * (2 * TPB) + 2 * TPB)
                    nc.vector.tensor_copy(top_e[:, :, :], top_idx[:, :, 0:TOPK])
                    step(nc.vector.tensor_tensor(top_sum[:, :], top_val[:, :, 0], top_val[:, :, 1], ALU.add), 5)
                    for c in range(TOPK):
                        nc.vector.tensor_tensor(onehot[:, :, c, :],
                                                iota8[:, :].unsqueeze(1).broadcast_to([P, TPB, E]),
                                                top_e[:, :, c].unsqueeze(2).broadcast_to([P, TPB, E]), ALU.is_equal)
                    nc.vector.tensor_scalar(top_sum[:, :], top_sum[:, :], 1e-8, None, ALU.add)
                    step(nc.vector.tensor_copy(top_w[:, :, :], top_val[:, :, 0:TOPK]), 6)
                    nc.vector.tensor_tensor(count[:, :, :], onehot[:, :, 0, :], onehot[:, :, 1, :],
                                            ALU.add).then_inc(s_count, 1)
                if r == 11:
                    step(nc.vector.reciprocal(top_sum[:, :], top_sum[:, :]), 7)
                    nc.vector.tensor_tensor(top_w[:, :, :], top_w[:, :, :],
                                            top_sum[:, :].unsqueeze(2).broadcast_to([P, TPB, TOPK]), ALU.mult)
                if r == 12:
                    dve.wait_ge(s_prefix, b + 1)
                    dve.wait_ge(s_place, b + 1)
                    counts = OUT[:, 0:(TPB + 1) * E].rearrange("p (t e) -> p t e", e=E)
                    step(nc.vector.tensor_tensor(prefix[:, :, :], counts[:, 0:TPB, :],
                                                 placed[:, :].unsqueeze(1).broadcast_to([P, TPB, E]), ALU.add), 8)
                    nc.vector.tensor_tensor(placed[:, :], placed[:, :], counts[:, TPB, :], ALU.add).then_inc(s_place, 1)
                if r == 13:
                    step(nc.vector.tensor_tensor(picked[:, :, :, :], onehot[:, :, :, :],
                                                 prefix[:, :, :].unsqueeze(2).broadcast_to([P, TPB, TOPK, E]),
                                                 ALU.mult), 9)
                    step(nc.vector.tensor_reduce(position[:, :, :], picked[:, :, :, :], AX, ALU.add), 10)
                if r == 14:
                    nc.vector.tensor_scalar(valid[:, :, :], position[:, :, :], float(CAP), None, ALU.is_lt)
                    nc.vector.tensor_scalar(slot_f[:, :, :], top_e[:, :, :], float(CAP), None, ALU.mult)
                    step(nc.vector.tensor_scalar(position[:, :, :], position[:, :, :], float(CAP - 1), None, ALU.min), 11)
                if r == 15:
                    nc.vector.tensor_tensor(item_w[:, bass.ds(b * (TPB * TOPK), TPB * TOPK)]
                                            .rearrange("p (t c) -> p t c", c=TOPK),
                                            top_w[:, :, :], valid[:, :, :], ALU.mult)
                    nc.vector.tensor_scalar(skip_f[:, :, :], valid[:, :, :], -NOWHERE, NOWHERE, ALU.mult, ALU.add)
                    step(nc.vector.tensor_tensor(slot_f[:, :, :], slot_f[:, :, :], position[:, :, :], ALU.add), 12)
                    nc.vector.tensor_copy(gather_idx[:, bass.ds(b * (TPB * TOPK), TPB * TOPK)]
                                          .rearrange("p (t c) -> p t c", c=TOPK), slot_f[:, :, :])
                    nc.vector.tensor_tensor(scatter_idx[:, :].rearrange("p (t c) -> p t c", c=TOPK), slot_f[:, :, :],
                                            skip_f[:, :, :], ALU.add).then_inc(s_routed, 1)

            dve.wait_ge(s_const, 4)
            all_periods(dve, dve_step, dve_route)

            def slots_split(e):
                for c in range(3):
                    n0, n1 = c * 512, min(KC * CAP, c * 512 + 512)
                    dve.wait_ge(s_slots_hi, e * 3 + (c + 1))
                    nc.vector.tensor_tensor(slots_lo[:, n0:n1], banks[c][:, 0:n1 - n0],
                                            slots_hi[:, n0:n1].bitcast(F32), ALU.subtract).then_inc(s_slots_lo, 1)

            def hidden_split(e):
                if later(e):
                    dve.wait_ge(s_expert, e * SLOTT)
                for c in range(HC):
                    n = e * HC + c
                    dve.wait_ge(s_relu, n + 1)
                    nc.vector.tensor_copy(hidden_hi[:, c, :], hidden[c % 2][:, :]).then_inc(s_hidden_hi, 1)
                    dve.wait_ge(s_hidden_hi, n + 1)
                    nc.vector.tensor_tensor(hidden_lo[:, c, :], hidden[c % 2][:, :],
                                            hidden_hi[:, c, :].bitcast(F32), ALU.subtract).then_inc(s_hidden_lo, 1)

            def rows_out(e):
                if later(e):
                    dve.wait_ge(s_expert_out, e * 16)
                for s in range(SLOTT):
                    dve.wait_ge(s_expert, e * SLOTT + (s + 1))
                    nc.vector.tensor_tensor(expert_sb[:, s, :], FFN2[s][:, 0:D],
                                            b2_sb[:, bass.ds(e, 1), :].rearrange("p a d -> p (a d)"),
                                            ALU.add).then_inc(s_expert_sb, 1)

            slots_split(0)
            hidden_split(0)
            slots_split(1)
            rows_out(0)
            hidden_split(1)
            with dve.Fori(1, E - 1) as e:
                slots_split(e + 1)
                rows_out(e)
                hidden_split(e + 1)
            rows_out(E - 1)
            for b in range(B):
                i = b % 2
                dve.wait_ge(s_gathered[i], 16 * TPB * TOPK * (b // 2 + 1))
                if later(16 * (b // 2)):
                    dve.wait_ge(s_out[i], 16 * (b // 2))
                for t in range(TPB):
                    n = b * TPB + t
                    nc.vector.scalar_tensor_tensor(combined[i][:, t, :], gathered[i][:, 2 * t, :],
                                                   item_w[:, 2 * n:2 * n + 1], x_sb[:, n, :],
                                                   ALU.mult, ALU.add).then_inc(s_first, 1)
                dve.wait_ge(s_first, TPB * (b + 1))
                for t in range(TPB):
                    n = b * TPB + t
                    ins = nc.vector.scalar_tensor_tensor(combined[i][:, t, :], gathered[i][:, 2 * t + 1, :],
                                                         item_w[:, 2 * n + 1:2 * n + 2], combined[i][:, t, :],
                                                         ALU.mult, ALU.add)
                ins.then_inc(s_combined, 1)

        @block.tensor
        def _(pe):
            start_ahead(pe, "pe")
            pe.wait_ge(s_const, 2)
            def turn_norm(b):
                for t in range(TPB):
                    n = b * TPB + t
                    pe.wait_ge(s_norm, n + 1)
                    if n >= 2:
                        pe.wait_ge(s_xT, n - 1)
                    for kc in range(KC):
                        ins = nc.tensor.transpose(SCORE[t % 2][:, kc * P:(kc + 1) * P],
                                                  xn[:, t % 2, kc * P:(kc + 1) * P], identity[:, :])
                    ins.then_inc(s_norm_turned, 1)

            def project(g, t, routed=None):
                q = g * TPB + t
                if t == 0:
                    pe.wait_ge(s_xcur, (g // NKV) * 16 + 16)
                    if later(2 * g - 4):
                        pe.wait_ge(s_residual, 2 * g - 4 + 1)
                if later(q):
                    pe.wait_ge(s_proj_out, q)
                if t == 3 and routed is not None:
                    pe.wait_ge(s_shifted, routed + 1)
                for kc in range(KC):
                    ins = nc.tensor.matmul(PROJ[:, 0:GW], xcur[:, kc, t * P:(t + 1) * P],
                                           w_sb[:, kc, bass.ds(g % NKV, 1), :].rearrange("p a n -> p (a n)"),
                                           start=(kc == 0), stop=(kc == KC - 1))
                ins.then_inc(s_proj, 1)

            def turn_qk(g, t, routed=None):
                q = g * TPB + t
                pe.wait_ge(s_split, q + 1)
                if later(q):
                    pe.wait_ge(s_q_ready, q)
                    pe.wait_ge(s_k_ready, q)
                if t == 0 and later(2 * g - 2):
                    pe.wait_ge(s_recip_sb, 2 * g - 2)
                if t == 3 and later(2 * g - 1):
                    pe.wait_ge(s_recip_sb, 2 * g - 1)
                if t == 0 and routed is not None:
                    pe.wait_ge(s_x2T, routed * 2 + 2)
                src = qk_split[t % 2]
                for h in range(QM):
                    nc.tensor.transpose(QTURN[:, h * P:(h + 1) * P].bitcast(F32R), src[:, h * P:(h + 1) * P],
                                        identity_r[:, :])
                for s in range(2):
                    ins = nc.tensor.transpose(KTURN[:, s * P:(s + 1) * P].bitcast(F32R),
                                              src[:, (QM + s) * P:(QM + s + 1) * P], identity_r[:, :])
                ins.then_inc(s_qk_turned, 1)

            def pe_step(n, g, j, follow, routed):
                if 0 <= n < UNITS:
                    h, t = divmod(n, TPB)
                    U = g * UNITS + n
                    if n == 0:
                        pe.wait_ge(s_q_ready, (g + 1) * TPB)
                        pe.wait_ge(s_k_ready, (g + 1) * TPB)
                    if later(U - 1):
                        pe.wait_ge(s_neg_max, U - 1)
                    for s in range(2):
                        ins = nc.tensor.matmul(SCORE[n % 2][:, :], q_st[j][:, h, t * P:(t + 1) * P],
                                               k_st[j][:, s, :], start=(s == 0), stop=(s == 1))
                    ins.then_inc(s_scores, 1)
                u = n - LAG
                if 0 <= u < UNITS:
                    pe.wait_ge(s_probs, g * UNITS + u + 1)
                    if later(g * (UNITS // 2) + u // 2):
                        pe.wait_ge(s_probs_t[u % 2], g * (UNITS // 2) + u // 2)
                    for c in range(TPB):
                        ins = nc.tensor.transpose(TURN[u % 2][:, c * P:(c + 1) * P],
                                                  probs[u % RING][:, c * P:(c + 1) * P], identity[:, :])
                    ins.then_inc(s_turned, 1)
                if n in PROJ_AT:
                    project(g, PROJ_AT[n], routed)
                if n in WIDEN_AT:
                    p = WIDEN_AT[n]
                    pe.wait_ge(s_recip, 2 * g + p + 1)
                    if follow:
                        pe.wait_ge(s_q_ready, (g + 1) * TPB + (3 if p == 0 else 4))
                    if later(2 * g + p):
                        pe.wait_ge(s_recip_sb, 2 * g + p)
                    for t in range(TPB):
                        ins = nc.tensor.transpose(QTURN[:, t * P:(t + 1) * P],
                                                  recip_cols[:, t, :, :].rearrange("p h d -> p (h d)"),
                                                  identity[:, :])
                    ins.then_inc(s_recip_wide, 1)
                if n in PV_AT:
                    p, c = PV_AT[n]
                    if c == 0:
                        for s in range(2):
                            pe.wait_ge(s_probs_t[s], g * (UNITS // 2) + 4 * (p + 1))
                        pe.wait_ge(s_v, g + 1)
                        if later(2 * g + p):
                            pe.wait_ge(s_heads, 2 * g + p + 1)
                        if routed is not None:
                            pe.wait_ge(s_place, routed + 2)
                    for hh in range(2):
                        ins = nc.tensor.matmul(OUT[hh * HD:(hh + 1) * HD, :], v_sb[j][:, c, :],
                                               probs_t[2 * p + hh][:, c, :], start=(c == 0), stop=(c == TPB - 1))
                    if c == TPB - 1:
                        ins.then_inc(s_pv, 1)
                if n in Y_AT:
                    half = Y_AT[n]
                    pe.wait_ge(s_heads, 2 * g + 2 + 1)
                    if half == 0 and follow == 2:
                        pe.wait_ge(s_proj_out, (g + 3) * TPB)
                    if later(2 * g + half):
                        pe.wait_ge(s_residual, 2 * g + half + 1)
                    for tt in range(2):
                        t = 2 * half + tt
                        for p in range(PAIRS):
                            ins = nc.tensor.matmul(
                                PROJ[:, tt * D:(tt + 1) * D], heads[p][:, t * P:(t + 1) * P],
                                wo_sb[:, bass.ds((g % NKV) * PAIRS + p, 1), :].rearrange("p a n -> p (a n)"),
                                start=(p == 0), stop=(p == PAIRS - 1))
                    ins.then_inc(s_y, 1)
                if n in QK_AT:
                    turn_qk(g, QK_AT[n], routed)

            turn_norm(0)
            pe.wait_ge(s_w0_in, 16 * 3)
            project(0, 0)
            project(0, 1)
            turn_norm(1)
            project(0, 2)
            turn_qk(0, 0)
            turn_norm(2)
            project(0, 3)
            turn_qk(0, 1)
            turn_norm(3)
            turn_qk(0, 2)
            turn_qk(0, 3)
            pe.wait_ge(s_weights_in, 16 * 3 * KC)
            pe.wait_ge(s_wo_in, 16)
            pe.wait_ge(s_gate_in, 16)
            pe.wait_ge(s_const, 4)
            def pe_route(r, b, last):
                if r in (3, 4):
                    half = r - 3
                    pe.wait_ge(s_norm2, b * TPB + (2 * half + 2))
                    if half == 1:
                        pe.wait_ge(s_x2T, b * 2 + 1)
                    elif not last:
                        pe.wait_ge(s_k_ready, b * (NKV * TPB) + (NKV + 2) * TPB)
                    for m in range(2 * KC):
                        t, kc = 2 * half + m // KC, m % KC
                        ins = nc.tensor.transpose(KTURN[:, m * P:(m + 1) * P], xn2[:, t, kc * P:(kc + 1) * P],
                                                  identity[:, :])
                    ins.then_inc(s_norm2_turned, 1)
                if r == 6:
                    pe.wait_ge(s_x2T, b * 2 + 2)
                    if not last:
                        pe.wait_ge(s_proj_out, b * (NKV * TPB) + ((NKV + 2) * TPB + 3))
                    for t in range(TPB):
                        for kc in range(KC):
                            ins = nc.tensor.matmul(PROJ[:, t * E:(t + 1) * E], x2T[:, t * KC + kc, :],
                                                   gate_sb[:, kc, :], start=(kc == 0), stop=(kc == KC - 1))
                    ins.then_inc(s_logits, 1)
                if r == 11:
                    pe.wait_ge(s_count, b + 1)
                    if last:
                        pe.wait_ge(s_heads, 2 * GROUPS + 1)
                    else:
                        pe.wait_ge(s_heads, b * (2 * NKV) + (2 * (NKV + 1) + 1))
                    for t in range(TPB + 1):
                        for s in range(t):
                            ins = nc.tensor.matmul(OUT[:, t * E:(t + 1) * E], ones[:, :], count[:, s, :],
                                                   start=(s == 0), stop=(s == TPB - 1))
                        if t < TPB:
                            ins = nc.tensor.matmul(OUT[:, t * E:(t + 1) * E], before[:, :], count[:, t, :],
                                                   start=(t == 0), stop=True)
                    ins.then_inc(s_prefix, 1)

            all_periods(pe, pe_step, pe_route)

            pe.wait_ge(s_bias_in, 32)
            pe.wait_ge(s_shifted, B)
            nc.tensor.transpose(PROJ[:, 0:E * HC], b1_rows[:, :], identity[0:E * HC, 0:E * HC]).then_inc(s_b1_turned, 1)

            def turn_slots(e):
                pe.wait_ge(s_slots_in, e * 16 + 16)
                if later(e):
                    pe.wait_ge(s_slots_lo, e * 3)
                    pe.wait_ge(s_hidden, e * HC)
                for m in range(KC * SLOTT):
                    kc, s = divmod(m, SLOTT)
                    ins = nc.tensor.transpose(banks[m // 4][:, (m % 4) * P:(m % 4 + 1) * P],
                                              slots[:, s, kc * P:(kc + 1) * P], identity[:, :])
                    if m % 4 == 3 or m == KC * SLOTT - 1:
                        ins.then_inc(s_slots_turned, 1)

            W1X = [(w1_hi, slots_hi), (w1_hi, slots_lo), (w1_lo, slots_hi)]
            W2X = [(hidden_hi, w2_hi), (hidden_hi, w2_lo), (hidden_lo, w2_hi)]

            def to_hidden(e):
                pe.wait_ge(s_slots_lo, e * 3 + 3)
                pe.wait_ge(s_w1_lo, e + 1)
                for c in range(HC):
                    n = e * HC + c
                    if c < 2 and later(e):
                        pe.wait_ge(s_expert_sb, e * SLOTT - (3 if c == 0 else 1))
                    if later(n - 1):
                        pe.wait_ge(s_relu, n - 1)
                    for half in range(2):
                        for kc in range(KC):
                            for m, (w, a) in enumerate(W1X):
                                at = kc * CAP + half * HALF
                                ins = nc.tensor.matmul(banks[4 + 2 * (c % 2) + half][:, 0:HALF],
                                                       w[:, kc, c * P:(c + 1) * P], a[:, at:at + HALF],
                                                       start=(kc == 0 and m == 0), stop=(kc == KC - 1 and m == 2))
                    ins.then_inc(s_hidden, 1)

            def to_rows(e):
                pe.wait_ge(s_w2_lo, e + 1)
                pe.wait_ge(s_hidden_lo, e * HC + HC)
                if later(e):
                    pe.wait_ge(s_expert_sb, e * SLOTT)
                for s in range(SLOTT):
                    for c in range(HC):
                        for m, (a, w) in enumerate(W2X):
                            ins = nc.tensor.matmul(FFN2[s][:, 0:D], a[:, c, s * P:(s + 1) * P], w[:, c, :],
                                                   start=(c == 0 and m == 0), stop=(c == HC - 1 and m == 2))
                    ins.then_inc(s_expert, 1)

            turn_slots(0)
            pe.wait_ge(s_b1, 1)
            to_hidden(0)
            turn_slots(1)
            to_rows(0)
            with pe.Fori(1, E - 1) as e:
                to_hidden(e)
                turn_slots(e + 1)
                to_rows(e)
            to_hidden(E - 1)
            to_rows(E - 1)


def rope_tables():
    import numpy as np
    freq = (np.float32(1.0 / 1024.0) ** np.linspace(0.0, 1.0, RH, dtype=np.float32)).astype(np.float32)
    theta = np.arange(L, dtype=np.float32)[:, None] * freq[None, :]
    tables = np.stack([np.cos(theta), np.sin(theta), -np.sin(theta)], axis=1).astype(np.float32)
    return np.ascontiguousarray(tables.reshape(TPB, P, 3, RH).transpose(1, 0, 2, 3))


_INS = ["L0_attn_x", "L0_attn_W_qkv", "L0_attn_W_out", "L0_attn_s", "L0_ffn_gating_w",
        "L0_ffn_w1", "L0_ffn_b1", "L0_ffn_w2", "L0_ffn_b2"]


def kernel(**inputs):
    import numpy as np
    import concourse.bacc as bacc
    from concourse.bass_utils import run_bass_kernel_spmd

    nc = bacc.Bacc("TRN2", target_bir_lowering=False, num_devices=1)
    arrays, args = {}, []
    for name in _INS:
        a = np.ascontiguousarray(inputs[name])
        arrays[f"in_{name}"] = a
        args.append(nc.dram_tensor(f"in_{name}", a.shape, F32, kind="ExternalInput").ap())
    arrays["rope"] = rope_tables()
    args.append(nc.dram_tensor("rope", arrays["rope"].shape, F32, kind="ExternalInput").ap())
    args.append(nc.dram_tensor("out", (B, L, D), F32, kind="ExternalOutput").ap())
    moe_layer(nc, *args)
    r = run_bass_kernel_spmd(nc, [arrays], core_ids=[0])
    return r.results[0]["out"]
```

```python
from contextlib import ExitStack

import concourse.bass as bass
from concourse import mybir
from concourse.alu_op_type import AluOpType as ALU

F32 = mybir.dt.float32
F32R = mybir.dt.float32r
U32 = mybir.dt.uint32
ACT = mybir.ActivationFunctionType
AX = mybir.AxisListType.X

P = 128
B, L, D = 4, 512, 256
T = B * L
TILES = T // P
TPB = L // P
KC = D // P
NKV, QM, HD = 8, 4, 64
NQ = NKV * QM
GROUPS = B * NKV
BAND = 64
GW = QM * HD + 2 * HD
RH = HD // 4
PAIRS = QM // 2
UNITS = QM * TPB
E, HID, CAP, TOPK = 8, 1024, 640, 2
HC = HID // P
SLOTT = CAP // P
HALF = CAP // 2
EPS = 1e-5
SCALE = HD ** -0.5
MASKED = -3.0e38
NOWHERE = 1.0e6
LAG = 4
CHUNK, RING5 = 2, 4
RING = 8


def moe_layer(nc, x, w_qkv, w_out, sink, gate_w, w1, b1, w2, b2, rope, out):
    ctx = ExitStack()
    with ctx:
        slot_rows = nc.dram_tensor("slot_rows", (E * CAP, D), F32, kind="Internal").ap()
        x_parts = nc.dram_tensor("x_parts", (B, P, 2 * KC * L), F32, kind="Internal").ap()
        expert_rows = nc.dram_tensor("expert_rows", (E * CAP, D), F32, kind="Internal").ap()

        def sem(name):
            return ctx.enter_context(nc.semaphore(name))

        def sb(name, shape, dt=F32, c=ctx):
            return c.enter_context(nc.sbuf_tensor(name, shape, dt))

        banks = [ctx.enter_context(nc.psum_tensor(f"bank{i}", [P, 512], F32)) for i in range(8)]
        FFN2 = banks[3:8]
        SCORE, TURN = banks[0:2], banks[2:4]
        OUT, PROJ, QTURN, KTURN = banks[4], banks[5], banks[6], banks[7]

        LN_TILES = TILES - TPB
        x_sb = sb("x_sb", [P, TILES, D])
        identity = sb("identity", [P, P])
        stats = sb("stats", [P, LN_TILES, 6])
        mean_var = sb("mean_var", [P, LN_TILES, 2])
        var_eps = sb("var_eps", [P, LN_TILES])
        std = sb("std", [P, LN_TILES])
        rstd0 = sb("rstd0", [P, LN_TILES])
        newton = sb("newton", [P, LN_TILES])
        rstd = sb("rstd", [P, LN_TILES])

        gate_sb = sb("gate_sb", [P, KC, E])
        xn2 = sb("xn2", [P, TPB, D])
        x2T = sb("x2T", [P, TPB * KC, P])
        before = sb("before", [P, P])
        ones = sb("ones", [P, P])
        iota8 = sb("iota8", [P, E])
        logit_max = sb("logit_max", [P, TPB])
        gates = sb("gates", [P, TPB, E])
        gate_sum = sb("gate_sum", [P, TPB])
        top_val = sb("top_val", [P, TPB, 8])
        top_idx = sb("top_idx", [P, TPB, 8], U32)
        top_e = sb("top_e", [P, TPB, TOPK])
        top_sum = sb("top_sum", [P, TPB])
        top_w = sb("top_w", [P, TPB, TOPK])
        onehot = sb("onehot", [P, TPB, TOPK, E])
        count = sb("count", [P, TPB, E])
        placed = sb("placed", [P, E])
        prefix = sb("prefix", [P, TPB, E])
        picked = sb("picked", [P, TPB, TOPK, E])
        position = sb("position", [P, TPB, TOPK])
        valid = sb("valid", [P, TPB, TOPK])
        slot_f = sb("slot_f", [P, TPB, TOPK])
        skip_f = sb("skip_f", [P, TPB, TOPK])
        scatter_idx = sb("scatter_idx", [P, TPB * TOPK], U32)
        gather_idx = sb("gather_idx", [P, TILES * TOPK], U32)
        item_w = sb("item_w", [P, TILES * TOPK])

        s_const = sem("s_const")
        s_x_in = [sem(f"s_x_in{b}") for b in range(B)]
        s_w0_in = sem("s_w0_in")
        s_wo_in = sem("s_wo_in")
        s_sink_in = sem("s_sink_in")
        s_weights_in = sem("s_weights_in")
        s_weights2_in = sem("s_weights2_in")
        s_small_in = sem("s_small_in")
        s_gate_in = sem("s_gate_in")
        s_bias_in = sem("s_bias_in")
        s_rows_gone = sem("s_rows_gone")
        s_pool = sem("s_pool")
        s_hi = sem("s_hi")
        s_pool2 = sem("s_pool2")
        s_ln = sem("s_ln")
        s_sink = sem("s_sink")
        s_denom = sem("s_denom")
        s_place = sem("s_place")
        s_route = sem("s_route")
        s_top = sem("s_top")
        s_first = sem("s_first")
        s_passed = sem("s_passed")
        s_var = sem("s_var")
        s_std = sem("s_std")
        s_norm = sem("s_norm")
        s_norm_turned = sem("s_norm_turned")
        s_xT_hi = sem("s_xT_hi")
        s_xT_lo = sem("s_xT_lo")
        s_parts_out = sem("s_parts_out")
        s_wq_hi = sem("s_wq_hi")
        s_wq_lo = sem("s_wq_lo")
        s_xcur = sem("s_xcur")
        s_batch = sem("s_batch")
        s_proj = sem("s_proj")
        s_proj_out = sem("s_proj_out")
        s_v = sem("s_v")
        s_split = sem("s_split")
        s_qk_turned = sem("s_qk_turned")
        s_q_ready = sem("s_q_ready")
        s_k_ready = sem("s_k_ready")
        s_scores = sem("s_scores")
        s_neg_max = sem("s_neg_max")
        s_probs = sem("s_probs")
        s_turned = sem("s_turned")
        s_probs_t = [sem("s_probs_t_even"), sem("s_probs_t_odd")]
        s_sink_arg = sem("s_sink_arg")
        s_sink_exp = sem("s_sink_exp")
        s_recip = sem("s_recip")
        s_recip_wide = sem("s_recip_wide")
        s_recip_sb = sem("s_recip_sb")
        s_pv = sem("s_pv")
        s_heads = sem("s_heads")
        s_y = sem("s_y")
        s_residual = sem("s_residual")
        s_zero_rows = sem("s_zero_rows")
        s_norm2 = sem("s_norm2")
        s_norm2_turned = sem("s_norm2_turned")
        s_x2T = sem("s_x2T")
        s_logits = sem("s_logits")
        s_shifted = sem("s_shifted")
        s_gate_exp = sem("s_gate_exp")
        s_count = sem("s_count")
        s_prefix = sem("s_prefix")
        s_routed = sem("s_routed")
        s_scattered = sem("s_scattered")
        s_w1_in = sem("s_w1_in")
        s_w2_in = sem("s_w2_in")
        s_b1_turned = sem("s_b1_turned")
        s_b1 = sem("s_b1")
        s_w1_hi = sem("s_w1_hi")
        s_w1_lo = sem("s_w1_lo")
        s_w2_hi = sem("s_w2_hi")
        s_w2_lo = sem("s_w2_lo")
        s_slots_in = sem("s_slots_in")
        s_slots_turned = sem("s_slots_turned")
        s_slots_hi = sem("s_slots_hi")
        s_slots_lo = sem("s_slots_lo")
        s_hidden = sem("s_hidden")
        s_relu = sem("s_relu")
        s_hidden_hi = sem("s_hidden_hi")
        s_hidden_lo = sem("s_hidden_lo")
        s_expert = sem("s_expert")
        s_expert_sb = sem("s_expert_sb")
        s_expert_out = sem("s_expert_out")
        s_last_out = sem("s_last_out")
        s_gathered = [sem(f"s_gathered{i}") for i in range(RING5)]
        s_combined = sem("s_combined")
        s_out = [sem(f"s_out{i}") for i in range(RING5)]

        actx = ExitStack()
        w_qkv_hi = sb("w_qkv_hi", [P, KC, NKV, GW], F32R, c=actx)
        w_qkv_lo = sb("w_qkv_lo", [P, KC, NKV, GW], F32R, c=actx)
        wo_sb = sb("wo_sb", [P, NQ // 2, D], c=actx)
        xcur = sb("xcur", [P, 2, KC, L], F32R, c=actx)
        MASK_W = 2 * L - P
        mask = sb("mask", [P, MASK_W], c=actx)
        rope_sb = sb("rope_sb", [P, TPB, 3, RH], c=actx)
        identity_r = sb("identity_r", [P, P], F32R, c=actx)
        sink_all = sb("sink_all", [P, NQ], c=actx)
        sink_cur = sb("sink_cur", [P, 2, QM], c=actx)
        sink_neg = sb("sink_neg", [P, 2, QM], c=actx)
        qk_sb = [sb(f"qk_sb{i}", [P, GW - HD], c=actx) for i in range(2)]
        v_next = sb("v_next", [P, TPB, HD], c=actx)
        rot_a = sb("rot_a", [P, (QM + 1) * 2 * RH], c=actx)
        rot_b = sb("rot_b", [P, (QM + 1) * 2 * RH], c=actx)
        qk_split = [sb(f"qk_split{i}", [P, 6 * P], F32R, c=actx) for i in range(2)]
        q_st = [sb(f"q_st{i}", [P, QM, L], F32R, c=actx) for i in range(2)]
        k_st = [sb(f"k_st{i}", [P, 2, L], F32R, c=actx) for i in range(2)]
        v_sb = [sb(f"v_sb{i}", [P, TPB, HD], c=actx) for i in range(2)]
        probs_ring = sb("probs_ring", [P, RING, L], c=actx)
        probs = [probs_ring[:, i, :] for i in range(RING)]
        probs_t = [sb(f"probs_t{h}", [P, TPB, L], c=actx) for h in range(QM)]
        neg_max = [sb(f"neg_max{i}", [P, UNITS], c=actx) for i in range(2)]
        sums = [sb(f"sums{i}", [P, UNITS], c=actx) for i in range(2)]
        sink_arg = sb("sink_arg", [P, UNITS], c=actx)
        sink_exp = sb("sink_exp", [P, UNITS], c=actx)
        denom = sb("denom", [P, UNITS], c=actx)
        recip = sb("recip", [P, UNITS], c=actx)
        recip_cols = sb("recip_cols", [P, TPB, 2, HD], c=actx)
        recip_sb = sb("recip_sb", [P, L], c=actx)
        heads_sb = sb("heads_sb", [P, PAIRS, L], c=actx)
        heads = [heads_sb[:, p, :] for p in range(PAIRS)]
        actx.close()

        mctx = ExitStack()
        w1_raw = sb("w1_raw", [P, KC, HID], c=mctx)
        w2_raw = sb("w2_raw", [P, HC, D], c=mctx)
        b1_rows = sb("b1_rows", [E * HC, P], c=mctx)
        b1_sb = sb("b1_sb", [P, E, HC], c=mctx)
        b1_cur = sb("b1_cur", [P, HC], c=mctx)
        b2_sb = sb("b2_sb", [P, E, D], c=mctx)
        w1_hi = sb("w1_hi", [P, KC, HID], F32R, c=mctx)
        w1_lo = sb("w1_lo", [P, KC, HID], F32R, c=mctx)
        w2_hi = sb("w2_hi", [P, HC, D], F32R, c=mctx)
        w2_lo = sb("w2_lo", [P, HC, D], F32R, c=mctx)
        slots = sb("slots", [P, SLOTT, D], c=mctx)
        slots_hi = sb("slots_hi", [P, KC * CAP], F32R, c=mctx)
        slots_lo = sb("slots_lo", [P, KC * CAP], F32R, c=mctx)
        hidden = [sb(f"hidden{i}", [P, CAP], c=mctx) for i in range(2)]
        hidden_hi = sb("hidden_hi", [P, HC, CAP], F32R, c=mctx)
        hidden_lo = sb("hidden_lo", [P, HC, CAP], F32R, c=mctx)
        expert_sb = sb("expert_sb", [P, SLOTT, D], c=mctx)
        gathered = [sb(f"gathered{i}", [P, CHUNK * TOPK, D], c=mctx) for i in range(RING5)]
        combined = [sb(f"combined{i}", [P, CHUNK, D], c=mctx) for i in range(RING5)]
        mctx.close()

        AHEAD = {
            "pe": [s_pv, s_y],
            "pool": [s_rows_gone, s_batch],
            "dve": [s_heads, s_residual],
        }

        def start_ahead(eng, name):
            for s in AHEAD[name]:
                eng.sem_inc(s, 1)

        def later(n):
            return not isinstance(n, int) or n > 0

        def plain(eng):
            eng.sem_inc(s_passed, 1)

        x_rows = x.rearrange("b (t p) d -> p (b t) d", p=P)
        out_rows = out.rearrange("b (t p) d -> p (b t) d", p=P)

        PROJ_AT = {-15: 0, -13: 1, -11: 2, -7: 3}
        QK_AT = {-11: 0, -8: 1, -5: 2, -2: 3}
        PV_AT = {13 + 8 * p + c: (p, c) for p in range(PAIRS) for c in range(TPB)}
        SINK_AT = {8: 0, 16: 1}
        RECIP_AT = {11: 0, 17: 1}
        WIDEN_AT = {13: 0, 19: 1}
        HEADS_AT = {17: 0, 25: 1}
        Y_AT = {27: 0, 29: 1}

        def period(step, g, j, prev=True, cur=True, nxt=True, also=None, b=None):
            for n in range(UNITS):
                if cur:
                    step(n, g, j, int(nxt), b)
                if prev:
                    step(n + UNITS, g - 1, 1 - j, int(cur) + int(nxt), b)
                if nxt:
                    step(n - UNITS, g + 1, 1 - j, 2, b)
                if also:
                    also(n)

        ROUTE_FROM = -4
        TURN2_AT = {3: 0, 6: 1}
        LOGITS_AT = 7
        COUNT_AT = 12

        def all_periods(eng, step, route):
            def route_first(b):
                return lambda n: route(n - UNITS, b, False) if n - UNITS >= ROUTE_FROM else None

            period(step, 0, 0, prev=False)
            period(step, 1, 1)
            with eng.Fori(0, B - 1) as b:
                with eng.Fori(0, NKV // 2 - 1) as i:
                    for k in range(2):
                        period(step, b * NKV + i * 2 + (k + 2), k)
                period(step, b * NKV + NKV, 0, also=route_first(b))
                period(step, b * NKV + (NKV + 1), 1, also=lambda n: route(n, b, False), b=b)
            with eng.Fori(0, NKV // 2 - 2) as i:
                for k in range(2):
                    period(step, i * 2 + (GROUPS - NKV + 2 + k), k)
            period(step, GROUPS - 2, 0)
            period(step, GROUPS - 1, 1, nxt=False)
            period(step, GROUPS, 0, cur=False, nxt=False, also=route_first(B - 1))
            for r in range(UNITS):
                route(r, B - 1, True)

        def xT_part(n, part):
            b, t = divmod(n, TPB)
            if b == 0:
                return xcur[:, part, :, t * P:(t + 1) * P]
            return probs_t[b][:, part * KC:(part + 1) * KC, t * P:(t + 1) * P].bitcast(F32R)

        NORM_BANKS = banks[0:4]
        WQ_RAW = [(first, buf.rearrange("p h q -> p (h q)")[:, 0:KC * n * GW]
                   .rearrange("p (c s n) -> p c s n", c=KC, n=GW), n)
                  for first, buf, n in [(0, heads_sb[:, :, :], 1), (1, probs_ring[:, :, :], 5), (6, probs_t[0][:, :, :], 2)]]

        def wq_raw(a, b):
            for first, view, n in WQ_RAW:
                if first <= a and b <= first + n:
                    return view[:, :, a - first:b - first, :]

        block = ctx.enter_context(nc.Block())

        @block.sync
        def _(sp):
            sp.dma_start(x_sb[:, 0:TPB, :], x_rows[:, 0:TPB, :]).then_inc(s_x_in[0], 16)
            QW, KW = NQ * HD, NKV * HD
            parts = [(0, QM * HD, 0), (QM * HD, HD, QW), (QM * HD + HD, HD, QW + KW)]
            def load_wq(first, n, done):
                for kc in range(KC):
                    rows = w_qkv[kc * P:(kc + 1) * P, :]
                    for at, width, col in parts:
                        a = col + first * width
                        sp.dma_start(wq_raw(first, first + n)[:, kc, :, at:at + width],
                                     rows[:, a:a + n * width].rearrange("p (g n) -> p g n", n=width)).then_inc(done, 16)

            load_wq(0, 1, s_w0_in)
            sp.dma_start(rope_sb[:, :, :, :], rope).then_inc(s_small_in, 16)
            sp.wait_ge(s_w0_in, 16 * 3 * KC)
            for b in range(1, B):
                sp.dma_start(x_sb[:, b * TPB:(b + 1) * TPB, :],
                             x_rows[:, b * TPB:(b + 1) * TPB, :]).then_inc(s_x_in[b], 16)
            load_wq(1, 5, s_weights_in)
            load_wq(6, 2, s_weights2_in)
            sp.dma_start(sink_all[:, :], sink.rearrange("a k m -> a (k m)").partition_broadcast(P)
                         .rearrange("p a n -> p (a n)")).then_inc(s_sink_in, 16)
            sp.dma_start(wo_sb[:, :, :], w_out.rearrange("(c p) n -> p c n", p=P)).then_inc(s_wo_in, 16)
            sp.dma_start(gate_sb[:, :, :], gate_w.rearrange("(c p) e -> p c e", p=P)).then_inc(s_gate_in, 16)
            for b in range(1, B):
                sp.wait_ge(s_xT_hi, (b + 1) * TPB)
                sp.wait_ge(s_xT_lo, (b + 1) * TPB)
                sp.dma_start(x_parts[b], probs_t[b][:, :, :].rearrange("p c q -> p (c q)")).then_inc(s_parts_out, 16)
            sp.wait_ge(s_const, 3)
            sp.dma_start(slot_rows.rearrange("(p j) d -> p j d", p=P),
                         x2T[:, 0:KC, :].rearrange("p c d -> p (c d)").unsqueeze(1)
                         .broadcast_to([P, E * CAP // P, D])).then_inc(s_zero_rows, 16)
            sp.wait_ge(s_proj, GROUPS * TPB)
            sp.dma_start(w1_raw[:, :, :], w1[0].rearrange("(c p) n -> p c n", p=P)).then_inc(s_w1_in, 16)
            sp.dma_start(w2_raw[:, :, :], w2[0].rearrange("(c p) n -> p c n", p=P)).then_inc(s_w2_in, 16)
            sp.wait_ge(s_residual, 2 * GROUPS + 1)
            sp.dma_start(b1_rows[:, :], b1.rearrange("e (c p) -> (e c) p", p=P)).then_inc(s_bias_in, 16)
            sp.dma_start(b2_sb[:, :, :].rearrange("p e d -> p (e d)"),
                         b2.rearrange("(a e) d -> a (e d)", a=1).partition_broadcast(P)
                         .rearrange("p a n -> p (a n)")).then_inc(s_bias_in, 16)
            sp.wait_ge(s_scattered, 16 * TILES * TOPK)
            def slots_in(e):
                sp.dma_start(slots[:, :, :], slot_rows[bass.ds(e * CAP, CAP), :]
                             .rearrange("(p j) d -> p j d", j=SLOTT)).then_inc(s_slots_in, 16)

            def rows_out(e):
                sp.wait_ge(s_expert_sb, SLOTT * e + SLOTT)
                sp.dma_start(expert_rows[bass.ds(e * CAP, CAP), :].rearrange("(p j) d -> p j d", j=SLOTT),
                             expert_sb[:, :, :]).then_inc(s_expert_out, 16)

            slots_in(0)
            with sp.Fori(0, E - 1) as e:
                sp.wait_ge(s_slots_turned, e * 3 + 3)
                slots_in(e + 1)
                sp.wait_ge(s_w1_hi, e + 1)
                sp.wait_ge(s_w1_lo, e + 1)
                sp.dma_start(w1_raw[:, :, :], w1[bass.ds(e + 1, 1)].rearrange("a (c p) n -> p (a c) n", p=P)
                             ).then_inc(s_w1_in, 16)
                sp.wait_ge(s_w2_hi, e + 1)
                sp.wait_ge(s_w2_lo, e + 1)
                sp.dma_start(w2_raw[:, :, :], w2[bass.ds(e + 1, 1)].rearrange("a (c p) n -> p (a c) n", p=P)
                             ).then_inc(s_w2_in, 16)
                rows_out(e)
            for s in range(SLOTT):
                sp.wait_ge(s_expert_sb, SLOTT * (E - 1) + s + 1)
                sp.dma_start(expert_rows[(E - 1) * CAP:E * CAP, :].rearrange("(p j) d -> p j d", j=SLOTT)[:, s, :],
                             expert_sb[:, s, :]).then_inc(s_last_out, 16)
            with sp.Fori(0, TILES // CHUNK // RING5) as turn:
                for i in range(RING5):
                    sp.wait_ge(s_combined, turn * RING5 + (i + 1))
                    sp.dma_start(out_rows[:, bass.ds((turn * RING5 + i) * CHUNK, CHUNK), :],
                                 combined[i][:, :, :]).then_inc(s_out[i], 16)
            for i in range(RING5):
                sp.wait_ge(s_out[i], 16 * (TILES // CHUNK // RING5))

        @block.gpsimd
        def _(pool):
            start_ahead(pool, "pool")
            steps = [0]

            def own(ins):
                steps[0] += 1
                ins.then_inc(s_pool, 1)
                pool.wait_ge(s_pool, steps[0])

            own(nc.gpsimd.memset(identity[:, :], 0.0))
            nc.gpsimd.affine_select(out=identity[:, :], in_=identity[:, :], compare_op=ALU.not_equal, fill=1.0,
                                    base=0, pattern=[[-1, P]], channel_multiplier=1).then_inc(s_const, 1)
            pool.wait_ge(s_const, 1)
            nc.gpsimd.tensor_copy(identity_r[:, :], identity[:, :]).then_inc(s_const, 1)
            nc.gpsimd.memset(x2T[:, 0:KC, :], 0.0)
            own(nc.gpsimd.memset(mask[:, :], MASKED))
            own(nc.gpsimd.affine_select(out=mask[:, :], in_=mask[:, :], compare_op=ALU.is_ge, fill=0.0,
                                        base=L - P, pattern=[[-1, MASK_W]], channel_multiplier=1))
            nc.gpsimd.affine_select(out=mask[:, :], in_=mask[:, :], compare_op=ALU.is_ge, fill=0.0,
                                    base=BAND - 1 - (L - P), pattern=[[1, MASK_W]],
                                    channel_multiplier=-1).then_inc(s_const, 1)
            before_group = steps[0]
            ROT_STEPS = 4

            def split(g, t):
                q = g * TPB + t
                pool.wait_ge(s_proj_out, q + 1)
                if later(q - 1):
                    pool.wait_ge(s_qk_turned, q - 1)
                src, dst = qk_sb[t % 2], qk_split[t % 2]
                NH = QM + 1
                rot = src[:, :].rearrange("p (h j r) -> p h j r", j=2, r=HD // 2)[:, :, :, 0:RH]
                cos = rope_sb[:, t, 0, :].unsqueeze(1).unsqueeze(1)
                sin = rope_sb[:, t, 1, :].unsqueeze(1)
                nsin = rope_sb[:, t, 2, :].unsqueeze(1)
                a = rot_a[:, :].rearrange("p (h j r) -> p h j r", j=2, r=RH)
                c = rot_b[:, :].rearrange("p (h j r) -> p h j r", j=2, r=RH)
                base = before_group + q * ROT_STEPS
                nc.gpsimd.tensor_tensor(a, rot, cos.broadcast_to([P, NH, 2, RH]), ALU.mult).then_inc(s_pool, 1)
                nc.gpsimd.tensor_tensor(c[:, :, 0, :], rot[:, :, 1, :], sin.broadcast_to([P, NH, RH]),
                                        ALU.mult).then_inc(s_pool, 1)
                nc.gpsimd.tensor_tensor(c[:, :, 1, :], rot[:, :, 0, :], nsin.broadcast_to([P, NH, RH]),
                                        ALU.mult).then_inc(s_pool, 1)
                pool.wait_ge(s_pool, base + 3)
                nc.gpsimd.tensor_tensor(rot, a, c, ALU.add).then_inc(s_pool, 1)
                pool.wait_ge(s_pool, base + 4)
                plain(pool)
                q_in = src[:, 0:QM * HD].rearrange("p (h d) -> p h d", d=HD)
                k_in = src[:, QM * HD:NH * HD].unsqueeze(1).broadcast_to([P, 2, HD])
                q_out = dst[:, 0:QM * P].rearrange("p (h s d) -> p h s d", s=2, d=HD)
                k_hi = dst[:, QM * P:(QM + 1) * P].rearrange("p (s d) -> p s d", d=HD)
                k_lo = dst[:, (QM + 1) * P:(QM + 2) * P].rearrange("p (s d) -> p s d", d=HD)
                nc.gpsimd.tensor_copy(q_out[:, :, 0, :], q_in)
                nc.gpsimd.tensor_copy(k_hi, k_in).then_inc(s_hi, 1)
                pool.wait_ge(s_hi, q + 1)
                nc.gpsimd.tensor_tensor(q_out[:, :, 1, :], q_in, q_out[:, :, 0, :].bitcast(F32), ALU.subtract)
                nc.gpsimd.tensor_tensor(k_lo, k_in, k_hi.bitcast(F32), ALU.subtract).then_inc(s_split, 1)

            def keep_v(g, j):
                if later(2 * g - 2):
                    pool.wait_ge(s_pv, 2 * g - 2 + 1)
                plain(pool)
                nc.gpsimd.tensor_copy(v_sb[j][:, :, :], v_next[:, :, :]).then_inc(s_v, 1)

            pool.wait_ge(s_small_in, 16)
            def group(g, j, routed=None):
                for t in range(TPB):
                    split(g, t)
                keep_v(g, j)
                if routed is not None:
                    for t in range(TPB):
                        scatter(routed, t)

            def scatter(b, t):
                if t == 0:
                    pool.wait_ge(s_routed, b + 1)
                plain(pool)
                for k in range(TOPK):
                    c = t * TOPK + k
                    nc.gpsimd.indirect_dma_start(
                        slot_rows, bass.IndirectOffsetOnAxis(ap=scatter_idx[:, c:c + 1], axis=0),
                        xn2[:, t, :], None, bounds_check=E * CAP - 1, oob_is_err=False).then_inc(s_scattered, 16)

            group(0, 0)
            nc.gpsimd.memset(ones[:, :], 1.0)
            nc.gpsimd.iota(iota8[:, :], pattern=[[1, E]], base=0, channel_multiplier=0,
                           allow_small_or_imprecise_dtypes=True)
            nc.gpsimd.memset(before[:, :], 1.0).then_inc(s_pool2, 1)
            pool.wait_ge(s_pool2, 1)
            nc.gpsimd.affine_select(out=before[:, :], in_=before[:, :], compare_op=ALU.is_gt, fill=0.0, base=0,
                                    pattern=[[1, P]], channel_multiplier=-1).then_inc(s_const, 1)
            for g in range(1, 4):
                group(g, g % 2)
            pool.wait_ge(s_parts_out, 16 * (B - 1))
            pool.wait_ge(s_zero_rows, 16)
            with pool.Fori(0, B - 1) as b:
                with pool.Fori(0, NKV // 2 - 2) as i:
                    for j in range(2):
                        group(b * NKV + i * 2 + (j + 4), j)
                pool.wait_ge(s_proj, b * (NKV * TPB) + NKV * TPB)
                plain(pool)
                nc.gpsimd.dma_start(xcur[:, :, :, :].rearrange("p a c q -> p (a c q)"),
                                    x_parts[bass.ds(b + 1, 1)].rearrange("a p n -> p (a n)")).then_inc(s_xcur, 16)
                pool.wait_ge(s_xcur, b * 16 + 16)
                pool.sem_inc(s_batch, 1)
                for j in range(3):
                    group(b * NKV + (NKV + j), j % 2)
                group(b * NKV + (NKV + 3), 1, routed=b)
                pool.wait_ge(s_scattered, b * (16 * TPB * TOPK) + 16 * TPB * TOPK)
                pool.sem_inc(s_rows_gone, 1)
            with pool.Fori(0, NKV // 2 - 2) as i:
                for j in range(2):
                    group(i * 2 + (GROUPS - NKV + 4 + j), j)
            for t in range(TPB):
                scatter(B - 1, t)
            with pool.Fori(0, E) as e:
                pool.wait_ge(s_w1_hi, e + 1)
                nc.gpsimd.tensor_tensor(w1_lo[:, :, :], w1_raw[:, :, :], w1_hi[:, :, :].bitcast(F32),
                                        ALU.subtract).then_inc(s_w1_lo, 1)
                pool.wait_ge(s_w2_hi, e + 1)
                nc.gpsimd.tensor_tensor(w2_lo[:, :, :], w2_raw[:, :, :], w2_hi[:, :, :].bitcast(F32),
                                        ALU.subtract).then_inc(s_w2_lo, 1)
            pool.wait_ge(s_expert_out, 16 * (E - 1))
            pool.wait_ge(s_last_out, 16 * SLOTT)
            for q in range(TILES // CHUNK):
                i = q % RING5
                if later(q - RING5 + 1):
                    pool.wait_ge(s_combined, q - RING5 + 1)
                for c in range(CHUNK * TOPK):
                    n = q * CHUNK * TOPK + c
                    nc.gpsimd.indirect_dma_start(
                        gathered[i][:, c, :], None, expert_rows,
                        bass.IndirectOffsetOnAxis(ap=gather_idx[:, n:n + 1], axis=0)).then_inc(s_gathered[i], 16)

        @block.scalar
        def _(act):
            def root(n):
                act.wait_ge(s_var, n + 1)
                nc.scalar.activation(std[:, 0:(TPB, LN_TILES)[n]], var_eps[:, 0:(TPB, LN_TILES)[n]],
                                     ACT.Sqrt).then_inc(s_std, 1)

            def norm_hi(n):
                act.wait_ge(s_norm_turned, n + 1)
                nc.scalar.activation(xT_part(n, 0), NORM_BANKS[n % 4][:, 0:D].rearrange("p (c q) -> p c q", c=KC),
                                     ACT.Copy).then_inc(s_xT_hi, 1)

            def wq_hi(a, b):
                nc.scalar.activation(w_qkv_hi[:, :, a:b, :], wq_raw(a, b), ACT.Copy).then_inc(s_wq_hi, 1)

            def proj_out(g, t):
                q = g * TPB + t
                act.wait_ge(s_proj, q + 1)
                if later(q - 1):
                    act.wait_ge(s_split, q - 1)
                if t == 0 and later(g):
                    act.wait_ge(s_v, g)
                nc.scalar.activation(qk_sb[t % 2][:, :], PROJ[:, 0:GW - HD], ACT.Copy)
                nc.scalar.activation(v_next[:, t, :], PROJ[:, GW - HD:GW], ACT.Copy).then_inc(s_proj_out, 1)

            def k_out(g, j, t):
                act.wait_ge(s_qk_turned, g * TPB + t + 1)
                nc.scalar.activation(k_st[j][:, :, t * P:(t + 1) * P],
                                     KTURN[:, 0:2 * P].rearrange("p (s q) -> p s q", s=2),
                                     ACT.Copy).then_inc(s_k_ready, 1)

            def act_step(n, g, j, follow, routed):
                if n in PROJ_AT:
                    proj_out(g, PROJ_AT[n])
                if n in QK_AT:
                    k_out(g, j, QK_AT[n])
                if n - 1 in WIDEN_AT:
                    p = WIDEN_AT[n - 1]
                    act.wait_ge(s_recip_wide, 2 * g + p + 1)
                    if later(2 * g + p):
                        act.wait_ge(s_heads, 2 * g + p + 1)
                    nc.scalar.activation(recip_sb[:, :], QTURN[:, :], ACT.Copy).then_inc(s_recip_sb, 1)
                if 0 <= n < UNITS:
                    act.wait_ge(s_neg_max, g * UNITS + n + 1)
                    nc.scalar.activation(probs[n % RING][:, :], probs[n % RING][:, :], ACT.Exp,
                                         bias=neg_max[j][:, n:n + 1], scale=-1.0,
                                         accum_out=sums[j][:, n:n + 1]).then_inc(s_probs, 1)
                u = n - LAG
                if 0 <= u < UNITS and u % 2 == 1:
                    h, t = divmod(u, TPB)
                    act.wait_ge(s_turned, g * UNITS + u + 1)
                    if later(2 * g - 1 + h // 2):
                        act.wait_ge(s_pv, 2 * g - 1 + h // 2 + 1)
                    elif u < 2:
                        act.wait_ge(s_parts_out, 16 * (B - 1))
                    nc.scalar.activation(probs_t[h][:, :, t * P:(t + 1) * P],
                                         TURN[1][:, :].rearrange("p (c q) -> p c q", c=TPB),
                                         ACT.Copy).then_inc(s_probs_t[1], 1)
                if n in SINK_AT:
                    p = SINK_AT[n]
                    act.wait_ge(s_sink_arg, 2 * g + p + 1)
                    nc.scalar.activation(sink_exp[:, 8 * p:8 * p + 8], sink_arg[:, 8 * p:8 * p + 8],
                                         ACT.Exp).then_inc(s_sink_exp, 1)

            act.wait_ge(s_w0_in, 16 * 3 * KC)
            wq_hi(0, 1)
            root(0)
            for n in range(TPB):
                norm_hi(n)
            proj_out(0, 0)
            proj_out(0, 1)
            root(1)
            proj_out(0, 2)
            k_out(0, 0, 0)
            act.wait_ge(s_weights_in, 16 * 3 * KC)
            wq_hi(1, 2)
            for n in range(TPB, 2 * TPB):
                norm_hi(n)
            wq_hi(2, 6)
            proj_out(0, 3)
            k_out(0, 0, 1)
            for n in range(2 * TPB, 3 * TPB):
                norm_hi(n)
            act.wait_ge(s_weights2_in, 16 * 3 * KC)
            wq_hi(6, 8)
            k_out(0, 0, 2)
            for n in range(3 * TPB, 4 * TPB):
                norm_hi(n)
            k_out(0, 0, 3)

            def act_route(r, b, last):
                if r == 0:
                    act.wait_ge(s_var, b + 3)
                    nc.scalar.activation(std[:, 0:TPB], var_eps[:, 0:TPB], ACT.Sqrt).then_inc(s_std, 1)
                if r == min(TURN2_AT):
                    act.wait_ge(s_zero_rows, 16)
                if r in TURN2_AT:
                    half = TURN2_AT[r]
                    act.wait_ge(s_norm2_turned, b * 2 + half + 1)
                    nc.scalar.activation(x2T[:, half * 4:half * 4 + 4, :],
                                         KTURN[:, :].rearrange("p (c q) -> p c q", c=4),
                                         ACT.Copy).then_inc(s_x2T, 1)
                if r == LOGITS_AT + 1:
                    act.wait_ge(s_shifted, b + 1)
                    nc.scalar.activation(gates[:, :, :], gates[:, :, :], ACT.Exp).then_inc(s_gate_exp, 1)

            all_periods(act, act_step, act_route)
            act.wait_ge(s_residual, 2 * GROUPS + 1)
            act.wait_ge(s_b1_turned, 1)
            nc.scalar.activation(b1_sb[:, :, :], PROJ[:, 0:E * HC].rearrange("p (e c) -> p e c", e=E),
                                 ACT.Copy).then_inc(s_b1, 1)
            act.wait_ge(s_b1, 1)

            def w1_split(e):
                act.wait_ge(s_w1_in, e * 16 + 16)
                if later(e):
                    act.wait_ge(s_hidden, e * HC)
                nc.scalar.activation(w1_hi[:, :, :], w1_raw[:, :, :], ACT.Copy).then_inc(s_w1_hi, 1)
                if later(e):
                    act.wait_ge(s_relu, e * HC)
                nc.scalar.activation(b1_cur[:, :], b1_sb[:, bass.ds(e, 1), :].rearrange("p a c -> p (a c)"),
                                     ACT.Copy).then_inc(s_b1, 1)

            def w2_split(e):
                act.wait_ge(s_w2_in, e * 16 + 16)
                if later(e):
                    act.wait_ge(s_expert, e * SLOTT)
                nc.scalar.activation(w2_hi[:, :, :], w2_raw[:, :, :], ACT.Copy).then_inc(s_w2_hi, 1)

            def slots_split(e):
                for c in range(3):
                    act.wait_ge(s_slots_turned, e * 3 + (c + 1))
                    n0, n1 = c * 512, min(KC * CAP, c * 512 + 512)
                    nc.scalar.activation(slots_hi[:, n0:n1], banks[c][:, 0:n1 - n0],
                                         ACT.Copy).then_inc(s_slots_hi, 1)

            def relus(e, with_w2):
                act.wait_ge(s_b1, e + 2)
                for c in range(HC):
                    n = e * HC + c
                    act.wait_ge(s_hidden, n + 1)
                    if later(n - 1):
                        act.wait_ge(s_hidden_lo, n - 1)
                    for half in range(2):
                        ins = nc.scalar.activation(hidden[c % 2][:, half * HALF:(half + 1) * HALF],
                                                   banks[4 + 2 * (c % 2) + half][:, 0:HALF], ACT.Relu,
                                                   bias=b1_cur[:, c:c + 1])
                    ins.then_inc(s_relu, 1)
                    if c == 1 and with_w2:
                        w2_split(e)

            w1_split(0)
            w2_split(0)
            slots_split(0)
            relus(0, False)
            with act.Fori(1, E) as e:
                slots_split(e)
                w1_split(e)
                relus(e, True)

        @block.vector
        def _(dve):
            start_ahead(dve, "dve")
            LN_STEPS = [0, 2 * TPB + 5, 2 * TPB + 5 + 2 * LN_TILES + 5]

            def layernorm(n, first, tiles):
                k = LN_STEPS[n] + 2 * tiles
                for t in range(tiles):
                    if t % TPB == 0:
                        dve.wait_ge(s_x_in[(first + t) // TPB], 16)
                    nc.vector.bn_stats(stats[:, t, :], x_sb[:, first + t, :]).then_inc(s_ln, 1)
                    dve.wait_ge(s_ln, LN_STEPS[n] + 2 * t + 1)
                    nc.vector.bn_aggr(mean_var[:, t, :], stats[:, t, :]).then_inc(s_ln, 1)
                dve.wait_ge(s_ln, k)
                nc.vector.tensor_scalar(var_eps[:, 0:tiles], mean_var[:, 0:tiles, 1], EPS, None, ALU.add).then_inc(s_var, 1)
                dve.wait_ge(s_std, n + 1)
                nc.vector.reciprocal(rstd0[:, 0:tiles], std[:, 0:tiles]).then_inc(s_ln, 1)
                dve.wait_ge(s_ln, k + 1)
                nc.vector.tensor_tensor(newton[:, 0:tiles], rstd0[:, 0:tiles], rstd0[:, 0:tiles], ALU.mult).then_inc(s_ln, 1)
                dve.wait_ge(s_ln, k + 2)
                nc.vector.tensor_tensor(newton[:, 0:tiles], newton[:, 0:tiles], var_eps[:, 0:tiles],
                                        ALU.mult).then_inc(s_ln, 1)
                dve.wait_ge(s_ln, k + 3)
                nc.vector.tensor_scalar(newton[:, 0:tiles], newton[:, 0:tiles], -0.5, 1.5,
                                        ALU.mult, ALU.add).then_inc(s_ln, 1)
                dve.wait_ge(s_ln, k + 4)
                nc.vector.tensor_tensor(rstd[:, 0:tiles], rstd0[:, 0:tiles], newton[:, 0:tiles], ALU.mult).then_inc(s_ln, 1)
                dve.wait_ge(s_ln, k + 5)

            def normalise(n, t):
                if n >= TPB:
                    dve.wait_ge(s_norm_turned, n - TPB + 1)
                nc.vector.tensor_scalar(xn2[:, n % TPB, :], x_sb[:, n, :], mean_var[:, t, 0:1],
                                        rstd[:, t:t + 1], ALU.subtract, ALU.mult).then_inc(s_norm, 1)

            def norm_lo(n):
                dve.wait_ge(s_xT_hi, n + 1)
                nc.vector.tensor_tensor(xT_part(n, 1), NORM_BANKS[n % 4][:, 0:D].rearrange("p (c q) -> p c q", c=KC),
                                        xT_part(n, 0).bitcast(F32), ALU.subtract).then_inc(s_xT_lo, 1)

            def wq_lo(a, b, n):
                dve.wait_ge(s_wq_hi, n)
                nc.vector.tensor_tensor(w_qkv_lo[:, :, a:b, :], wq_raw(a, b), w_qkv_hi[:, :, a:b, :].bitcast(F32),
                                        ALU.subtract).then_inc(s_wq_lo, 1)

            def q_out(g, j, t):
                dve.wait_ge(s_qk_turned, g * TPB + t + 1)
                nc.vector.tensor_copy(q_st[j][:, :, t * P:(t + 1) * P],
                                      QTURN[:, :].rearrange("p (h q) -> p h q", h=QM)).then_inc(s_q_ready, 1)

            def sinks(g, j):
                cols = sink_all[:, bass.ds((g % NKV) * QM, QM)]
                nc.vector.tensor_copy(sink_cur[:, j, :], cols).then_inc(s_sink, 1)
                nc.vector.tensor_scalar(sink_neg[:, j, :], cols, -1.0, None, ALU.mult).then_inc(s_sink, 1)

            def dve_step(n, g, j, follow, routed):
                if n == -1:
                    sinks(g, j)
                if 0 <= n < UNITS:
                    U = g * UNITS + n
                    h, t = divmod(n, TPB)
                    dve.wait_ge(s_scores, U + 1)
                    if n == 0:
                        dve.wait_ge(s_sink, 2 * g + 2)
                    if later(U - RING + 1):
                        dve.wait_ge(s_turned, U - RING + 1)
                    plain(dve)
                    nc.vector.tensor_tensor_reduce(
                        probs[n % RING][:, :], SCORE[n % 2][:, :], mask[:, L - P - t * P:2 * L - P - t * P], -SCALE,
                        sink_neg[:, j, h:h + 1], ALU.add, ALU.min, neg_max[j][:, n:n + 1]).then_inc(s_neg_max, 1)
                u = n - LAG
                if 0 <= u < UNITS and u % 2 == 0:
                    h, t = divmod(u, TPB)
                    dve.wait_ge(s_turned, g * UNITS + u + 1)
                    if later(2 * g - 1 + h // 2):
                        dve.wait_ge(s_pv, 2 * g - 1 + h // 2 + 1)
                    elif u < 2:
                        dve.wait_ge(s_parts_out, 16 * (B - 1))
                    nc.vector.tensor_copy(probs_t[h][:, :, t * P:(t + 1) * P],
                                          TURN[0][:, :].rearrange("p (c q) -> p c q", c=TPB)
                                          ).then_inc(s_probs_t[0], 1)
                if n in SINK_AT:
                    p = SINK_AT[n]
                    dve.wait_ge(s_neg_max, g * UNITS + 8 * p + 8)
                    nc.vector.tensor_tensor(
                        sink_arg[:, 8 * p:8 * p + 8].rearrange("p (h t) -> p h t", t=TPB),
                        neg_max[j][:, 8 * p:8 * p + 8].rearrange("p (h t) -> p h t", t=TPB),
                        sink_cur[:, j, 2 * p:2 * p + 2].unsqueeze(2).broadcast_to([P, 2, TPB]),
                        ALU.add).then_inc(s_sink_arg, 1)
                if n in RECIP_AT:
                    p = RECIP_AT[n]
                    dve.wait_ge(s_probs, g * UNITS + 8 * p + 8)
                    dve.wait_ge(s_sink_exp, 2 * g + p + 1)
                    nc.vector.tensor_tensor(denom[:, 8 * p:8 * p + 8], sums[j][:, 8 * p:8 * p + 8],
                                            sink_exp[:, 8 * p:8 * p + 8], ALU.add).then_inc(s_denom, 1)
                    dve.wait_ge(s_denom, 4 * g + 2 * p + 1)
                    nc.vector.reciprocal(recip[:, 8 * p:8 * p + 8], denom[:, 8 * p:8 * p + 8]).then_inc(s_denom, 1)
                    dve.wait_ge(s_denom, 4 * g + 2 * p + 2)
                    if later(2 * g + p):
                        dve.wait_ge(s_recip_wide, 2 * g + p)
                    nc.vector.tensor_copy(recip_cols[:, :, :, :],
                                          recip[:, 8 * p:8 * p + 8].rearrange("p (h t) -> p t h", t=TPB)
                                          .unsqueeze(3).broadcast_to([P, TPB, 2, HD])).then_inc(s_recip, 1)
                if n in HEADS_AT:
                    p = HEADS_AT[n]
                    dve.wait_ge(s_pv, 2 * g + p + 1 + 1)
                    dve.wait_ge(s_recip_sb, 2 * g + p + 1)
                    if later(2 * g):
                        dve.wait_ge(s_y, 2 * g + 1)
                    nc.vector.tensor_tensor(heads[p][:, :], OUT[:, :], recip_sb[:, :], ALU.mult).then_inc(s_heads, 1)
                if n - 1 in Y_AT:
                    half = Y_AT[n - 1]
                    dve.wait_ge(s_y, 2 * g + half + 1 + 1)
                    if later(2 * g):
                        dve.wait_ge(s_residual, 2 * g + 1)
                    rows = x_sb[:, bass.ds((g // NKV) * TPB + 2 * half, 2), :]
                    nc.vector.tensor_tensor(rows, rows, PROJ[:, :].rearrange("p (t d) -> p t d", t=2),
                                            ALU.add).then_inc(s_residual, 1)
                if n in QK_AT:
                    q_out(g, j, QK_AT[n])

            nc.vector.memset(placed[:, :], 0.0).then_inc(s_place, 1)
            layernorm(0, 0, TPB)
            for n in range(TPB):
                normalise(n, n)
            wq_lo(0, 1, 1)
            for n in range(TPB):
                norm_lo(n)
            layernorm(1, TPB, LN_TILES)
            for b in range(1, B):
                for n in range(b * TPB, b * TPB + TPB):
                    normalise(n, n - TPB)
                q_out(0, 0, b - 1)
                if b == 1:
                    wq_lo(1, 2, 2)
                if b == 3:
                    wq_lo(2, 6, 3)
                for n in range(b * TPB, b * TPB + TPB):
                    norm_lo(n)
            q_out(0, 0, 3)
            dve.wait_ge(s_sink_in, 16)
            sinks(0, 0)
            wq_lo(6, 8, 4)

            def dve_route(r, b, last):
                def step(ins, n):
                    ins.then_inc(s_route, 1)
                    dve.wait_ge(s_route, b * 14 + n)

                def ln(ins, n):
                    ins.then_inc(s_ln, 1)
                    dve.wait_ge(s_ln, b * 13 + (LN_STEPS[2] + n))

                if r < 0:
                    t = r - ROUTE_FROM
                    dve.wait_ge(s_residual, b * (2 * NKV) + (2 * NKV + t // 2))
                    plain(dve)
                    ln(nc.vector.bn_stats(stats[:, t, :], x_sb[:, bass.ds(b * TPB + t, 1), :]
                                          .rearrange("p a d -> p (a d)")), 2 * t + 1)
                    plain(dve)
                    nc.vector.bn_aggr(mean_var[:, t, :], stats[:, t, :]).then_inc(s_ln, 1)
                if r == 0:
                    dve.wait_ge(s_ln, b * 13 + (LN_STEPS[2] + 8))
                    nc.vector.tensor_scalar(var_eps[:, 0:TPB], mean_var[:, 0:TPB, 1], EPS, None, ALU.add).then_inc(s_var, 1)
                if r == 1:
                    dve.wait_ge(s_std, b + 3)
                    ln(nc.vector.reciprocal(rstd0[:, 0:TPB], std[:, 0:TPB]), 9)
                    ln(nc.vector.tensor_tensor(newton[:, 0:TPB], rstd0[:, 0:TPB], rstd0[:, 0:TPB], ALU.mult), 10)
                    ln(nc.vector.tensor_tensor(newton[:, 0:TPB], newton[:, 0:TPB], var_eps[:, 0:TPB], ALU.mult), 11)
                if r == 2:
                    ln(nc.vector.tensor_scalar(newton[:, 0:TPB], newton[:, 0:TPB], -0.5, 1.5, ALU.mult, ALU.add), 12)
                    ln(nc.vector.tensor_tensor(rstd[:, 0:TPB], rstd0[:, 0:TPB], newton[:, 0:TPB], ALU.mult), 13)
                    dve.wait_ge(s_rows_gone, b + 1)
                if r in (2, 3):
                    for t in (2 * r - 4, 2 * r - 3):
                        nc.vector.tensor_scalar(xn2[:, t, :],
                                                x_sb[:, bass.ds(b * TPB + t, 1), :].rearrange("p a d -> p (a d)"),
                                                mean_var[:, t, 0:1], rstd[:, t:t + 1],
                                                ALU.subtract, ALU.mult).then_inc(s_norm2, 1)
                if r == LOGITS_AT + 1:
                    dve.wait_ge(s_logits, b + 1)
                    logits = PROJ[:, 0:TPB * E].rearrange("p (t e) -> p t e", e=E)
                    step(nc.vector.tensor_reduce(logit_max[:, :], logits, AX, ALU.max), 1)
                    nc.vector.tensor_tensor(gates[:, :, :], logits,
                                            logit_max[:, :].unsqueeze(2).broadcast_to([P, TPB, E]),
                                            ALU.subtract).then_inc(s_shifted, 1)
                if r == LOGITS_AT + 2:
                    dve.wait_ge(s_gate_exp, b + 1)
                    step(nc.vector.tensor_reduce(gate_sum[:, :], gates[:, :, :], AX, ALU.add), 2)
                    step(nc.vector.reciprocal(gate_sum[:, :], gate_sum[:, :]), 3)
                    step(nc.vector.tensor_tensor(gates[:, :, :], gates[:, :, :],
                                                 gate_sum[:, :].unsqueeze(2).broadcast_to([P, TPB, E]), ALU.mult), 4)
                    plain(dve)
                    for t in range(TPB):
                        nc.vector.max(top_val[:, t, :], gates[:, t, :]).then_inc(s_top, 1)
                if r == LOGITS_AT + 3:
                    dve.wait_ge(s_top, b * (2 * TPB) + TPB)
                    plain(dve)
                    for t in range(TPB):
                        nc.vector.max_index(top_idx[:, t, :], top_val[:, t, :], gates[:, t, :]).then_inc(s_top, 1)
                    dve.wait_ge(s_top, b * (2 * TPB) + 2 * TPB)
                    step(nc.vector.tensor_copy(top_e[:, :, :], top_idx[:, :, 0:TOPK]), 5)
                if r == COUNT_AT - 1:
                    for c in range(TOPK):
                        ins = nc.vector.tensor_tensor(onehot[:, :, c, :],
                                                      iota8[:, :].unsqueeze(1).broadcast_to([P, TPB, E]),
                                                      top_e[:, :, c].unsqueeze(2).broadcast_to([P, TPB, E]), ALU.is_equal)
                    step(ins, 6)
                    nc.vector.tensor_tensor(count[:, :, :], onehot[:, :, 0, :], onehot[:, :, 1, :],
                                            ALU.add).then_inc(s_count, 1)
                if r == COUNT_AT:
                    step(nc.vector.tensor_tensor(top_sum[:, :], top_val[:, :, 0], top_val[:, :, 1], ALU.add), 7)
                    step(nc.vector.tensor_scalar(top_sum[:, :], top_sum[:, :], 1e-8, None, ALU.add), 8)
                    step(nc.vector.reciprocal(top_sum[:, :], top_sum[:, :]), 9)
                    nc.vector.tensor_tensor(top_w[:, :, :], top_val[:, :, 0:TOPK],
                                            top_sum[:, :].unsqueeze(2).broadcast_to([P, TPB, TOPK]), ALU.mult)
                if r == COUNT_AT + 1:
                    dve.wait_ge(s_prefix, b + 1)
                    dve.wait_ge(s_place, b + 1)
                    counts = KTURN[:, 0:(TPB + 1) * E].rearrange("p (t e) -> p t e", e=E)
                    step(nc.vector.tensor_tensor(prefix[:, :, :], counts[:, 0:TPB, :],
                                                 placed[:, :].unsqueeze(1).broadcast_to([P, TPB, E]), ALU.add), 10)
                    nc.vector.tensor_tensor(placed[:, :], placed[:, :], counts[:, TPB, :], ALU.add).then_inc(s_place, 1)
                if r == COUNT_AT + 1:
                    step(nc.vector.tensor_tensor(picked[:, :, :, :], onehot[:, :, :, :],
                                                 prefix[:, :, :].unsqueeze(2).broadcast_to([P, TPB, TOPK, E]),
                                                 ALU.mult), 11)
                    step(nc.vector.tensor_reduce(position[:, :, :], picked[:, :, :, :], AX, ALU.add), 12)
                if r == 14:
                    nc.vector.tensor_scalar(valid[:, :, :], position[:, :, :], float(CAP), None, ALU.is_lt)
                    nc.vector.tensor_scalar(slot_f[:, :, :], top_e[:, :, :], float(CAP), None, ALU.mult)
                    step(nc.vector.tensor_scalar(position[:, :, :], position[:, :, :], float(CAP - 1), None, ALU.min), 13)
                if r == 15:
                    nc.vector.tensor_tensor(item_w[:, bass.ds(b * (TPB * TOPK), TPB * TOPK)]
                                            .rearrange("p (t c) -> p t c", c=TOPK),
                                            top_w[:, :, :], valid[:, :, :], ALU.mult)
                    nc.vector.tensor_scalar(skip_f[:, :, :], valid[:, :, :], -NOWHERE, NOWHERE, ALU.mult, ALU.add)
                    step(nc.vector.tensor_tensor(slot_f[:, :, :], slot_f[:, :, :], position[:, :, :], ALU.add), 14)
                    nc.vector.tensor_copy(gather_idx[:, bass.ds(b * (TPB * TOPK), TPB * TOPK)]
                                          .rearrange("p (t c) -> p t c", c=TOPK), slot_f[:, :, :])
                    nc.vector.tensor_tensor(scatter_idx[:, :].rearrange("p (t c) -> p t c", c=TOPK), slot_f[:, :, :],
                                            skip_f[:, :, :], ALU.add).then_inc(s_routed, 1)

            dve.wait_ge(s_const, 4)
            all_periods(dve, dve_step, dve_route)

            def slots_split(e):
                for c in range(3):
                    n0, n1 = c * 512, min(KC * CAP, c * 512 + 512)
                    dve.wait_ge(s_slots_hi, e * 3 + (c + 1))
                    nc.vector.tensor_tensor(slots_lo[:, n0:n1], banks[c][:, 0:n1 - n0],
                                            slots_hi[:, n0:n1].bitcast(F32), ALU.subtract).then_inc(s_slots_lo, 1)

            def hidden_split(e):
                if later(e):
                    dve.wait_ge(s_expert, e * SLOTT)
                for c in range(HC):
                    n = e * HC + c
                    dve.wait_ge(s_relu, n + 1)
                    nc.vector.tensor_copy(hidden_hi[:, c, :], hidden[c % 2][:, :]).then_inc(s_hidden_hi, 1)
                    dve.wait_ge(s_hidden_hi, n + 1)
                    nc.vector.tensor_tensor(hidden_lo[:, c, :], hidden[c % 2][:, :],
                                            hidden_hi[:, c, :].bitcast(F32), ALU.subtract).then_inc(s_hidden_lo, 1)

            def rows_out(e):
                if later(e):
                    dve.wait_ge(s_expert_out, e * 16)
                for s in range(SLOTT):
                    dve.wait_ge(s_expert, e * SLOTT + (s + 1))
                    nc.vector.tensor_tensor(expert_sb[:, s, :], FFN2[s][:, 0:D],
                                            b2_sb[:, bass.ds(e, 1), :].rearrange("p a d -> p (a d)"),
                                            ALU.add).then_inc(s_expert_sb, 1)

            slots_split(0)
            hidden_split(0)
            slots_split(1)
            rows_out(0)
            hidden_split(1)
            with dve.Fori(1, E - 1) as e:
                slots_split(e + 1)
                rows_out(e)
                hidden_split(e + 1)
            rows_out(E - 1)
            for q in range(TILES // CHUNK):
                i, lap = q % RING5, q // RING5
                dve.wait_ge(s_gathered[i], 16 * CHUNK * TOPK * (lap + 1))
                if later(16 * lap):
                    dve.wait_ge(s_out[i], 16 * lap)
                for t in range(CHUNK):
                    n = q * CHUNK + t
                    nc.vector.scalar_tensor_tensor(combined[i][:, t, :], gathered[i][:, 2 * t, :],
                                                   item_w[:, 2 * n:2 * n + 1], x_sb[:, n, :],
                                                   ALU.mult, ALU.add).then_inc(s_first, 1)
                dve.wait_ge(s_first, CHUNK * (q + 1))
                for t in range(CHUNK):
                    n = q * CHUNK + t
                    ins = nc.vector.scalar_tensor_tensor(combined[i][:, t, :], gathered[i][:, 2 * t + 1, :],
                                                         item_w[:, 2 * n + 1:2 * n + 2], combined[i][:, t, :],
                                                         ALU.mult, ALU.add)
                ins.then_inc(s_combined, 1)

        @block.tensor
        def _(pe):
            start_ahead(pe, "pe")
            pe.wait_ge(s_const, 2)
            def turn_norm(n):
                pe.wait_ge(s_norm, n + 1)
                if n >= 4:
                    pe.wait_ge(s_xT_lo, n - 3)
                for kc in range(KC):
                    ins = nc.tensor.transpose(NORM_BANKS[n % 4][:, kc * P:(kc + 1) * P],
                                              xn2[:, n % TPB, kc * P:(kc + 1) * P], identity[:, :])
                ins.then_inc(s_norm_turned, 1)

            def project(g, t, routed=None):
                q = g * TPB + t
                if t == 0:
                    if isinstance(g, int) and g in (1, 2):
                        pe.wait_ge(s_wq_lo, 2 if g == 1 else 4)
                    if isinstance(g, int) and g < NKV:
                        pe.wait_ge(s_xT_lo, TPB)
                    else:
                        pe.wait_ge(s_batch, (g // NKV) + 1)
                    if later(2 * g - 4):
                        pe.wait_ge(s_residual, 2 * g - 4 + 1)
                if later(q):
                    pe.wait_ge(s_proj_out, q)
                if t == 3 and routed is not None:
                    pe.wait_ge(s_shifted, routed + 1)
                for kc in range(KC):
                    for m, (part, w) in enumerate([(0, w_qkv_hi), (0, w_qkv_lo), (1, w_qkv_hi)]):
                        ins = nc.tensor.matmul(PROJ[:, 0:GW], xcur[:, part, kc, t * P:(t + 1) * P],
                                               w[:, kc, bass.ds(g % NKV, 1), :].rearrange("p a n -> p (a n)"),
                                               start=(kc == 0 and m == 0), stop=(kc == KC - 1 and m == 2))
                ins.then_inc(s_proj, 1)

            def turn_qk(g, t, routed=None):
                q = g * TPB + t
                pe.wait_ge(s_split, q + 1)
                if later(q):
                    pe.wait_ge(s_q_ready, q)
                    pe.wait_ge(s_k_ready, q)
                if t == 0 and later(2 * g - 2):
                    pe.wait_ge(s_recip_sb, 2 * g - 2)
                if t == 3 and later(2 * g - 1):
                    pe.wait_ge(s_recip_sb, 2 * g - 1)
                if t in (0, 1) and routed is not None:
                    pe.wait_ge(s_x2T, routed * 2 + (t + 1))
                if t == 3 and routed is not None:
                    pe.wait_ge(s_place, routed + 2)
                src = qk_split[t % 2]
                for h in range(QM):
                    nc.tensor.transpose(QTURN[:, h * P:(h + 1) * P].bitcast(F32R), src[:, h * P:(h + 1) * P],
                                        identity_r[:, :])
                for s in range(2):
                    ins = nc.tensor.transpose(KTURN[:, s * P:(s + 1) * P].bitcast(F32R),
                                              src[:, (QM + s) * P:(QM + s + 1) * P], identity_r[:, :])
                ins.then_inc(s_qk_turned, 1)

            def pe_step(n, g, j, follow, routed):
                if 0 <= n < UNITS:
                    h, t = divmod(n, TPB)
                    U = g * UNITS + n
                    if n == 0:
                        pe.wait_ge(s_q_ready, (g + 1) * TPB)
                        pe.wait_ge(s_k_ready, (g + 1) * TPB)
                    if later(U - 1):
                        pe.wait_ge(s_neg_max, U - 1)
                    for s in range(2):
                        ins = nc.tensor.matmul(SCORE[n % 2][:, :], q_st[j][:, h, t * P:(t + 1) * P],
                                               k_st[j][:, s, :], start=(s == 0), stop=(s == 1))
                    ins.then_inc(s_scores, 1)
                u = n - LAG
                if 0 <= u < UNITS:
                    pe.wait_ge(s_probs, g * UNITS + u + 1)
                    if later(g * (UNITS // 2) + u // 2):
                        pe.wait_ge(s_probs_t[u % 2], g * (UNITS // 2) + u // 2)
                    for c in range(TPB):
                        ins = nc.tensor.transpose(TURN[u % 2][:, c * P:(c + 1) * P],
                                                  probs[u % RING][:, c * P:(c + 1) * P], identity[:, :])
                    ins.then_inc(s_turned, 1)
                if n in PROJ_AT:
                    project(g, PROJ_AT[n], routed)
                if n in WIDEN_AT:
                    p = WIDEN_AT[n]
                    pe.wait_ge(s_recip, 2 * g + p + 1)
                    if follow:
                        pe.wait_ge(s_q_ready, (g + 1) * TPB + (3 if p == 0 else 4))
                    if later(2 * g + p):
                        pe.wait_ge(s_recip_sb, 2 * g + p)
                    for t in range(TPB):
                        ins = nc.tensor.transpose(QTURN[:, t * P:(t + 1) * P],
                                                  recip_cols[:, t, :, :].rearrange("p h d -> p (h d)"),
                                                  identity[:, :])
                    ins.then_inc(s_recip_wide, 1)
                if n in PV_AT:
                    p, c = PV_AT[n]
                    if c == 0:
                        for s in range(2):
                            pe.wait_ge(s_probs_t[s], g * (UNITS // 2) + 4 * (p + 1))
                        pe.wait_ge(s_v, g + 1)
                        if later(2 * g + p):
                            pe.wait_ge(s_heads, 2 * g + p + 1)
                    for hh in range(2):
                        ins = nc.tensor.matmul(OUT[hh * HD:(hh + 1) * HD, :], v_sb[j][:, c, :],
                                               probs_t[2 * p + hh][:, c, :], start=(c == 0), stop=(c == TPB - 1))
                    if c == TPB - 1:
                        ins.then_inc(s_pv, 1)
                if n in Y_AT:
                    half = Y_AT[n]
                    pe.wait_ge(s_heads, 2 * g + 2 + 1)
                    if half == 0 and follow == 2:
                        pe.wait_ge(s_proj_out, (g + 3) * TPB)
                    if later(2 * g + half):
                        pe.wait_ge(s_residual, 2 * g + half + 1)
                    for tt in range(2):
                        t = 2 * half + tt
                        for p in range(PAIRS):
                            ins = nc.tensor.matmul(
                                PROJ[:, tt * D:(tt + 1) * D], heads[p][:, t * P:(t + 1) * P],
                                wo_sb[:, bass.ds((g % NKV) * PAIRS + p, 1), :].rearrange("p a n -> p (a n)"),
                                start=(p == 0), stop=(p == PAIRS - 1))
                    ins.then_inc(s_y, 1)
                if n in QK_AT:
                    turn_qk(g, QK_AT[n], routed)

            for n in range(TPB):
                turn_norm(n)
            pe.wait_ge(s_wq_lo, 1)
            for t in range(3):
                project(0, t)
            turn_qk(0, 0)
            for n in range(TPB, 2 * TPB):
                turn_norm(n)
            project(0, 3)
            turn_qk(0, 1)
            for n in range(2 * TPB, 3 * TPB):
                turn_norm(n)
            turn_qk(0, 2)
            for n in range(3 * TPB, 4 * TPB):
                turn_norm(n)
            turn_qk(0, 3)
            pe.wait_ge(s_wo_in, 16)
            pe.wait_ge(s_gate_in, 16)
            pe.wait_ge(s_const, 4)
            def pe_route(r, b, last):
                if r in TURN2_AT:
                    half = TURN2_AT[r]
                    pe.wait_ge(s_norm2, b * TPB + (2 * half + 2))
                    if not last:
                        pe.wait_ge(s_k_ready, b * (NKV * TPB) + ((NKV + 2) * TPB + half))
                    elif half == 1:
                        pe.wait_ge(s_x2T, b * 2 + 1)
                    for m in range(2 * KC):
                        t, kc = 2 * half + m // KC, m % KC
                        ins = nc.tensor.transpose(KTURN[:, m * P:(m + 1) * P], xn2[:, t, kc * P:(kc + 1) * P],
                                                  identity[:, :])
                    ins.then_inc(s_norm2_turned, 1)
                if r == LOGITS_AT:
                    pe.wait_ge(s_x2T, b * 2 + 2)
                    if not last:
                        pe.wait_ge(s_proj_out, b * (NKV * TPB) + ((NKV + 2) * TPB + 3))
                    for t in range(TPB):
                        for kc in range(KC):
                            ins = nc.tensor.matmul(PROJ[:, t * E:(t + 1) * E], x2T[:, t * KC + kc, :],
                                                   gate_sb[:, kc, :], start=(kc == 0), stop=(kc == KC - 1))
                    ins.then_inc(s_logits, 1)
                if r == COUNT_AT:
                    pe.wait_ge(s_count, b + 1)
                    if not last:
                        pe.wait_ge(s_k_ready, b * (NKV * TPB) + ((NKV + 2) * TPB + 3))
                    for t in range(TPB + 1):
                        for s in range(t):
                            ins = nc.tensor.matmul(KTURN[:, t * E:(t + 1) * E], ones[:, :], count[:, s, :],
                                                   start=(s == 0), stop=(s == TPB - 1))
                        if t < TPB:
                            ins = nc.tensor.matmul(KTURN[:, t * E:(t + 1) * E], before[:, :], count[:, t, :],
                                                   start=(t == 0), stop=True)
                    ins.then_inc(s_prefix, 1)

            all_periods(pe, pe_step, pe_route)

            pe.wait_ge(s_bias_in, 32)
            pe.wait_ge(s_shifted, B)
            nc.tensor.transpose(PROJ[:, 0:E * HC], b1_rows[:, :], identity[0:E * HC, 0:E * HC]).then_inc(s_b1_turned, 1)

            def turn_slots(e):
                pe.wait_ge(s_slots_in, e * 16 + 16)
                if later(e):
                    pe.wait_ge(s_slots_lo, e * 3)
                    pe.wait_ge(s_hidden, e * HC)
                for m in range(KC * SLOTT):
                    kc, s = divmod(m, SLOTT)
                    ins = nc.tensor.transpose(banks[m // 4][:, (m % 4) * P:(m % 4 + 1) * P],
                                              slots[:, s, kc * P:(kc + 1) * P], identity[:, :])
                    if m % 4 == 3 or m == KC * SLOTT - 1:
                        ins.then_inc(s_slots_turned, 1)

            W1X = [(w1_hi, slots_hi), (w1_hi, slots_lo), (w1_lo, slots_hi)]
            W2X = [(hidden_hi, w2_hi), (hidden_hi, w2_lo), (hidden_lo, w2_hi)]

            def to_hidden(e):
                pe.wait_ge(s_slots_lo, e * 3 + 3)
                pe.wait_ge(s_w1_lo, e + 1)
                for c in range(HC):
                    n = e * HC + c
                    if c < 2 and later(e):
                        pe.wait_ge(s_expert_sb, e * SLOTT - (2 if c == 0 else 0))
                    if later(n - 1):
                        pe.wait_ge(s_relu, n - 1)
                    for half in range(2):
                        for kc in range(KC):
                            for m, (w, a) in enumerate(W1X):
                                at = kc * CAP + half * HALF
                                ins = nc.tensor.matmul(banks[4 + 2 * (c % 2) + half][:, 0:HALF],
                                                       w[:, kc, c * P:(c + 1) * P], a[:, at:at + HALF],
                                                       start=(kc == 0 and m == 0), stop=(kc == KC - 1 and m == 2))
                    ins.then_inc(s_hidden, 1)

            def to_rows(e):
                pe.wait_ge(s_w2_lo, e + 1)
                for s in range(SLOTT):
                    for c in range(HC):
                        if s == 0:
                            pe.wait_ge(s_hidden_lo, e * HC + (c + 1))
                        for m, (a, w) in enumerate(W2X):
                            ins = nc.tensor.matmul(FFN2[s][:, 0:D], a[:, c, s * P:(s + 1) * P], w[:, c, :],
                                                   start=(c == 0 and m == 0), stop=(c == HC - 1 and m == 2))
                    ins.then_inc(s_expert, 1)

            turn_slots(0)
            pe.wait_ge(s_b1, 1)
            to_hidden(0)
            turn_slots(1)
            to_rows(0)
            with pe.Fori(1, E - 1) as e:
                to_hidden(e)
                turn_slots(e + 1)
                to_rows(e)
            to_hidden(E - 1)
            to_rows(E - 1)


def rope_tables():
    import numpy as np
    freq = (np.float32(1.0 / 1024.0) ** np.linspace(0.0, 1.0, RH, dtype=np.float32)).astype(np.float32)
    theta = np.arange(L, dtype=np.float32)[:, None] * freq[None, :]
    tables = np.stack([np.cos(theta), np.sin(theta), -np.sin(theta)], axis=1).astype(np.float32)
    return np.ascontiguousarray(tables.reshape(TPB, P, 3, RH).transpose(1, 0, 2, 3))


_INS = ["L0_attn_x", "L0_attn_W_qkv", "L0_attn_W_out", "L0_attn_s", "L0_ffn_gating_w",
        "L0_ffn_w1", "L0_ffn_b1", "L0_ffn_w2", "L0_ffn_b2"]


def kernel(**inputs):
    import numpy as np
    import concourse.bacc as bacc
    from concourse.bass_utils import run_bass_kernel_spmd

    nc = bacc.Bacc("TRN2", target_bir_lowering=False, num_devices=1)
    arrays, args = {}, []
    for name in _INS:
        a = np.ascontiguousarray(inputs[name])
        arrays[f"in_{name}"] = a
        args.append(nc.dram_tensor(f"in_{name}", a.shape, F32, kind="ExternalInput").ap())
    arrays["rope"] = rope_tables()
    args.append(nc.dram_tensor("rope", arrays["rope"].shape, F32, kind="ExternalInput").ap())
    args.append(nc.dram_tensor("out", (B, L, D), F32, kind="ExternalOutput").ap())
    moe_layer(nc, *args)
    r = run_bass_kernel_spmd(nc, [arrays], core_ids=[0])
    return r.results[0]["out"]
```
